# Optimizing a Trainium2 kernel written in Bass

```python
import numpy as np
import jax
import jax.numpy as jnp

def _softmax(x, axis=-1):
    return jax.nn.softmax(x, axis=axis)

def _gelu(x):
    return jax.nn.gelu(x, approximate=True)

def _silu(x):
    return jax.nn.silu(x)

def _sigmoid(x):
    return jax.nn.sigmoid(x)

def _layernorm(x, axis=-1, eps=1e-05):
    m = jnp.mean(x, axis=axis, keepdims=True)
    v = jnp.var(x, axis=axis, keepdims=True)
    return (x - m) / jnp.sqrt(v + eps)

def _scatter_add(tgt, idx, src, axis=0):
    return tgt.at[idx].add(src)

def _segment_sum(src, seg, n):
    return jax.ops.segment_sum(src, seg, n)
kernel_name = 'mk_seq_postln_d1_jaxref_r8_930bed'

def setup_inputs(seed: int=0):
    np.random.seed(seed)
    _w = jnp.asarray

    def _L0_attn_setup():
        import jax, jax.numpy as jnp
        import numpy as np
        MODEL_DIM = 128
        NUM_HEADS = 16
        D_K = MODEL_DIM // NUM_HEADS
        MAX_SEQ_LEN = 512

        def _xavier(key, shape):
            fan_in, fan_out = (shape[1], shape[0])
            limit = np.sqrt(6.0 / (fan_in + fan_out)).astype(np.float32)
            return jax.random.uniform(key, shape, jnp.float32, -limit, limit)
        key = jax.random.key(seed)
        ks = jax.random.split(key, 6)
        x = jax.random.normal(ks[0], (2, 256, MODEL_DIM), jnp.float32)
        wq = _xavier(ks[1], (MODEL_DIM, MODEL_DIM))
        wk = _xavier(ks[2], (MODEL_DIM, MODEL_DIM))
        wv = _xavier(ks[3], (MODEL_DIM, MODEL_DIM))
        wo = _xavier(ks[4], (MODEL_DIM, MODEL_DIM))
        bq = jnp.zeros((MODEL_DIM,), jnp.float32)
        bk = jnp.zeros((MODEL_DIM,), jnp.float32)
        bv = jnp.zeros((MODEL_DIM,), jnp.float32)
        bo = jnp.zeros((MODEL_DIM,), jnp.float32)
        half = D_K // 2
        theta = jnp.power(10000.0, jnp.arange(half, dtype=jnp.float32) * (-2.0 / D_K))
        angles = jnp.arange(MAX_SEQ_LEN, dtype=jnp.float32)[:, None] * theta[None, :]
        rot_cos = jnp.cos(angles)
        rot_sin = jnp.sin(angles)
        return {'x': x, 'wq': wq, 'bq': bq, 'wk': wk, 'bk': bk, 'wv': wv, 'bv': bv, 'wo': wo, 'bo': bo, 'rot_cos': rot_cos, 'rot_sin': rot_sin}
    _L0_attn_in = _L0_attn_setup()

    def _L0_ffn_setup():
        import jax, jax.numpy as jnp
        import numpy as np
        B, S, D, O, H, E, K = (4, 128, 128, 128, 256, 16, 4)
        key = jax.random.key(seed)
        ks = jax.random.split(key, 8)
        x = jax.random.normal(ks[0], (B, S, D), dtype=jnp.float32)
        w_gate = jax.random.normal(ks[1], (D, E), dtype=jnp.float32) * 0.01
        w_noise = jnp.zeros((D, E), dtype=jnp.float32)
        W1 = jax.random.normal(ks[2], (E, D, H), dtype=jnp.float32) * (1.0 / np.sqrt(D))
        b1 = jnp.zeros((E, H), dtype=jnp.float32)
        W2 = jax.random.normal(ks[3], (E, H, O), dtype=jnp.float32) * (1.0 / np.sqrt(H))
        b2 = jnp.zeros((E, O), dtype=jnp.float32)
        return {'x': x, 'w_gate': w_gate, 'w_noise': w_noise, 'W1': W1, 'b1': b1, 'W2': W2, 'b2': b2}
    _L0_ffn_in = _L0_ffn_setup()
    _d = {'L0_attn_x': _L0_attn_in['x'], 'L0_attn_wq': _L0_attn_in['wq'], 'L0_attn_bq': _L0_attn_in['bq'], 'L0_attn_wk': _L0_attn_in['wk'], 'L0_attn_bk': _L0_attn_in['bk'], 'L0_attn_wv': _L0_attn_in['wv'], 'L0_attn_bv': _L0_attn_in['bv'], 'L0_attn_wo': _L0_attn_in['wo'], 'L0_attn_bo': _L0_attn_in['bo'], 'L0_attn_rot_cos': _L0_attn_in['rot_cos'], 'L0_attn_rot_sin': _L0_attn_in['rot_sin'], 'L0_ffn_w_gate': _L0_ffn_in['w_gate'], 'L0_ffn_w_noise': _L0_ffn_in['w_noise'], 'L0_ffn_W1': _L0_ffn_in['W1'], 'L0_ffn_b1': _L0_ffn_in['b1'], 'L0_ffn_W2': _L0_ffn_in['W2'], 'L0_ffn_b2': _L0_ffn_in['b2']}
    _x0 = _d['L0_attn_x']
    _d['L0_attn_x'] = jax.random.normal(jax.random.fold_in(jax.random.key(seed), 1), (4, 512, 128), dtype=_x0.dtype)
    del _x0
    return _d

def reference(L0_attn_x, L0_attn_wq, L0_attn_bq, L0_attn_wk, L0_attn_bk, L0_attn_wv, L0_attn_bv, L0_attn_wo, L0_attn_bo, L0_attn_rot_cos, L0_attn_rot_sin, L0_ffn_w_gate, L0_ffn_w_noise, L0_ffn_W1, L0_ffn_b1, L0_ffn_W2, L0_ffn_b2):

    def _L0_attn_ref(x, wq, bq, wk, bk, wv, bv, wo, bo, rot_cos, rot_sin):
        import jax, jax.numpy as jnp
        import numpy as np
        MODEL_DIM = 128
        NUM_HEADS = 16
        D_K = MODEL_DIM // NUM_HEADS
        MAX_SEQ_LEN = 512

        def _xavier(key, shape):
            fan_in, fan_out = (shape[1], shape[0])
            limit = np.sqrt(6.0 / (fan_in + fan_out)).astype(np.float32)
            return jax.random.uniform(key, shape, jnp.float32, -limit, limit)
        b, t, m = x.shape
        h, d = (NUM_HEADS, m // NUM_HEADS)
        q = (x @ wq.T + bq).reshape(b, h, t, d)
        k = (x @ wk.T + bk).reshape(b, h, t, d)
        v = (x @ wv.T + bv).reshape(b, h, t, d)
        c = rot_cos[t]
        s = rot_sin[t]

        def rope(u):
            ur = u.reshape(b, h, t, d // 2, 2)
            re, im = (ur[..., 0], ur[..., 1])
            return jnp.stack([re * c - im * s, re * s + im * c], axis=-1).reshape(b, h, t, d)
        q, k = (rope(q), rope(k))
        scores = jnp.einsum('bhqd,bhkd->bhqk', q, k) / np.float32(np.sqrt(d))
        p = jax.nn.softmax(scores, axis=-1)
        o = jnp.einsum('bhqk,bhkd->bhqd', p, v)
        o = o.transpose(0, 2, 1, 3).reshape(b, t, m)
        return o @ wo.T + bo

    def _L0_ffn_ref(x, w_gate, w_noise, W1, b1, W2, b2):
        import jax, jax.numpy as jnp
        import numpy as np
        B, S, D, O, H, E, K = (4, 128, 128, 128, 256, 16, 4)
        logits = jnp.zeros((x.shape[0], x.shape[1], E), dtype=x.dtype).at[..., 1].set(100.0)
        top_vals, top_idx = jax.lax.top_k(logits, K)
        gates_k = jax.nn.softmax(top_vals, axis=-1)
        gates = jnp.einsum('bske,bsk->bse', jax.nn.one_hot(top_idx, E, dtype=x.dtype), gates_k)
        h = jax.nn.relu(jnp.einsum('bsd,edh->ebsh', x, W1) + b1[:, None, None, :])
        y = jnp.einsum('ebsh,eho->ebso', h, W2) + b2[:, None, None, :]
        out = jnp.einsum('ebso,bse->bso', y, gates)
        return out
    x = L0_attn_x
    x = _layernorm(x + _L0_attn_ref(x, L0_attn_wq, L0_attn_bq, L0_attn_wk, L0_attn_bk, L0_attn_wv, L0_attn_bv, L0_attn_wo, L0_attn_bo, L0_attn_rot_cos, L0_attn_rot_sin), axis=-1)
    x = _layernorm(x + _L0_ffn_ref(x, L0_ffn_w_gate, L0_ffn_w_noise, L0_ffn_W1, L0_ffn_b1, L0_ffn_W2, L0_ffn_b2), axis=-1)
    return x

_drawn_inputs = setup_inputs


def setup_inputs(seed=0):
    import zlib

    import numpy as np

    out = dict(_drawn_inputs(seed))
    spreads = {'L0_attn_bq': (0.0, 0.8),
     'L0_attn_bk': (0.0, 0.727),
     'L0_attn_bv': (0.0, 0.349),
     'L0_attn_bo': (0.0, 0.1),
     'L0_ffn_w_noise': (0.0, 0.1),
     'L0_ffn_b1': (0.0, 0.1),
     'L0_ffn_b2': (0.0, 0.1)}
    factors = {}
    for name, (base, spread) in spreads.items():
        noise = np.random.default_rng([zlib.crc32(name.encode()), seed]).standard_normal(out[name].shape)
        drawn = base * np.exp(spread * noise) if base else spread * noise
        out[name] = jnp.asarray(drawn.astype(out[name].dtype))
    for name, factor in factors.items():
        out[name] = (out[name] * factor).astype(out[name].dtype)
    return out
```

```python
from contextlib import ExitStack

import numpy as np

import concourse.bass as bass
from concourse import mybir

F32 = mybir.dt.float32
BF16 = mybir.dt.bfloat16
ALU = mybir.AluOpType
ACT = mybir.ActivationFunctionType
AX = mybir.AxisListType

B, T, D = 4, 512, 128
H, DK = 16, 8
E_SEL, HID = 1, 256
R, C = T // H, D // DK
TILES = T // 128
G = 4
N = B * G
HALF = T // 2
TERMS = 6
KS = TERMS * DK
KM = KS + 3
MROWS = 24
EPS = 1e-5


def half(u, rows):
    return slice(64 * u, 64 * u + rows)


def build_layer(nc, x, wq, bq, wk, bk, wv, bv, wo, bo, rot_cos, rot_sin, w1, b1, w2, b2, out):
    with ExitStack() as ctx:
        def sb(name, shape, dt=F32):
            return ctx.enter_context(nc.sbuf_tensor(name, shape, dt))

        def ps(name, shape, dt=F32):
            return ctx.enter_context(nc.psum_tensor(name, shape, dt))

        def sem(name):
            return ctx.enter_context(nc.semaphore(name))

        q_dram = nc.dram_tensor("q_dram", (B, 128, TERMS, T), BF16, kind="Internal").ap()
        k_dram = nc.dram_tensor("k_dram", (B, 128, TERMS, T), BF16, kind="Internal").ap()
        v_dram = nc.dram_tensor("v_dram", (B, T, D), F32, kind="Internal").ap()
        m_dram = nc.dram_tensor("m_dram", (G, 2, MROWS, 4, R), BF16, kind="Internal").ap()

        x_nat = sb("x_nat", [128, B, TILES, D])
        x_bo = sb("x_bo", [128, B, TILES, D])
        xT = sb("xT", [128, B, T])
        w_nat = sb("w_nat", [128, 4, 128])
        wo_pad = sb("wo_pad", [128, 2, 128])
        wT = sb("wT", [128, 5, 128])
        w1_sb = sb("w1_sb", [128, HID])
        w2_sb = sb("w2_sb", [128, 2, D])
        b1_sb = sb("b1_sb", [128, 2])
        bias_bc = sb("bias_bc", [128, 3, D])
        bqk = sb("bqk", [128, 2])
        rot = sb("rot", [1, 2, DK // 2])
        rot_sq = sb("rot_sq", [1, 2, DK // 2])
        rot_g = sb("rot_g", [1, DK // 2])
        g_row = sb("g_row", [1, C, DK // 2, 2])
        g_col = sb("g_col", [128, 1])
        bq_g = sb("bq_g", [128, 1])
        one = sb("one", [1, 1])
        ident = sb("ident", [128, 128])
        den_sel = sb("den_sel", [128, 128])
        ones = sb("ones", [16, HALF], BF16)
        qf = sb("qf", [128, 2, T])
        kf = sb("kf", [128, 2, T])
        q_res = sb("q_res", [128, T])
        k_res = sb("k_res", [128, T])
        q_parts = sb("q_parts", [128, 2, 3, T], BF16)
        k_parts = sb("k_parts", [128, 2, 3, T], BF16)
        v_nat = sb("v_nat", [128, 2, TILES, D])
        q_all = sb("q_all", [128, B, C, HALF], BF16)
        k_all = sb("k_all", [128, B, C, HALF], BF16)
        q_slot = sb("q_slot", [128, G, 2, T], BF16)
        k_slot = sb("k_slot", [128, G, 2, T], BF16)
        v_all = sb("v_all", [128, B, H, 4 * DK])
        v_slot = sb("v_slot", [128, G, 4, 4, 32])
        neg_max = sb("neg_max", [128, G, 2, 8])
        m_res = sb("m_res", [128, 2, 8])
        m_src = sb("m_src", [128, 2, 32], BF16)
        m_rows = sb("m_rows", [128, G, 2, 32], BF16)
        probs = sb("probs", [128, 2, 2, 2, T])
        y_raw = sb("y_raw", [128, T])
        y_rec = sb("y_rec", [128, T])
        y_norm = sb("y_norm", [128, 2, T])
        res = sb("res", [128, TILES, D])
        stats = sb("stats", [128, TILES, 6])
        mv = sb("mv", [128, TILES, 2])
        var_eps = sb("var_eps", [128, TILES])
        minus_half = sb("minus_half", [128, TILES])
        rstd = sb("rstd", [128, TILES])
        x1 = sb("x1", [128, TILES, D])
        x1_b2 = sb("x1_b2", [128, TILES, D])
        x1T = sb("x1T", [128, T])
        hidT = sb("hidT", [128, 2, T])
        x2 = sb("x2", [128, B, TILES, D])

        st_ps = ps("st_ps", [128, 2, 2, T])
        s_ps = ps("s_ps", [128, 2, T])
        o_ps = ps("o_ps", [128, T])
        mi_ps = ps("mi_ps", [128, T])

        ld_w = sem("ld_w")
        ld_small = sem("ld_small")
        ld_x = [sem(f"ld_x{b}") for b in range(B)]
        ld_ffn = sem("ld_ffn")
        ident_ok = sem("ident_ok")
        consts_ok = sem("consts_ok")
        rot_ok = sem("rot_ok")
        g_ps_ok = sem("g_ps_ok")
        g_ok = sem("g_ok")
        wT_ps_ok = sem("wT_ps_ok")
        wT_ok = sem("wT_ok")
        wo_pad_ok = sem("wo_pad_ok")
        xT_ps_ok = sem("xT_ps_ok")
        xT_ok = sem("xT_ok")
        qk_ps_ok = sem("qk_ps_ok")
        v_ps_ok = sem("v_ps_ok")
        qf_ok = sem("qf_ok")
        kf_ok = sem("kf_ok")
        v_nat_ok = sem("v_nat_ok")
        q_split = sem("q_split")
        k_split = sem("k_split")
        q_out = [sem(f"q_out{b}") for b in range(B)]
        k_out = [sem(f"k_out{b}") for b in range(B)]
        v_out = [sem(f"v_out{b}") for b in range(B)]
        qk_in = [sem(f"qk_in{b}") for b in range(B)]
        v_in = [sem(f"v_in{b}") for b in range(B)]
        ones_ok = sem("ones_ok")
        fill_in = sem("fill_in")
        x_bo_ok = sem("x_bo_ok")
        v_zero = sem("v_zero")
        scores_ready = sem("scores_ready")
        max_done = sem("max_done")
        split_step = sem("split_step")
        rows_ready = sem("rows_ready")
        rows_out = [sem(f"rows_out{q}") for q in range(G)]
        rows_in = [sem(f"rows_in{q}") for q in range(G)]
        st_ready = sem("st_ready")
        exp_done = sem("exp_done")
        pv_done = sem("pv_done")
        o_copied = sem("o_copied")
        den_ready = sem("den_ready")
        rec_done = sem("rec_done")
        y_ready = sem("y_ready")
        slots_first = sem("slots_first")
        slot_step = sem("slot_step")
        proj_ready = sem("proj_ready")
        res_done = sem("res_done")
        stats_done = sem("stats_done")
        mv_done = sem("mv_done")
        var_done = sem("var_done")
        rstd_done = sem("rstd_done")
        ln_done = sem("ln_done")
        x1b_done = sem("x1b_done")
        x1T_ps_ok = sem("x1T_ps_ok")
        x1T_ok = sem("x1T_ok")
        hid_ready = sem("hid_ready")
        relu_done = sem("relu_done")
        y2_ready = sem("y2_ready")
        stored = sem("stored")

        block = ctx.enter_context(nc.Block())
        Q_REPS = ((0, 0, 3), (1, 3, 2), (2, 5, 1))
        K_RUNS = ((0, 3), (3, 2), (5, 1))
        n_small = 2 + 2 + 3

        @block.sync
        def _(sp):
            for b in range(B):
                sp.dma_start(x_nat[:, b], x[b].rearrange("(t p) m -> p t m", p=128)).then_inc(ld_x[b], 16)
            for i, w in enumerate((bv, bo, b2[E_SEL])):
                sp.dma_start(bias_bc[:, i], w.partition_broadcast(128)).then_inc(ld_small, 16)
            sp.dma_start(w1_sb[:], w1[E_SEL]).then_inc(ld_ffn, 16)
            sp.dma_start(w2_sb[:], w2[E_SEL].rearrange("(m p) n -> p m n", p=128)).then_inc(ld_ffn, 16)
            for m in range(2):
                sp.dma_start(b1_sb[:, m:m + 1], b1[E_SEL, 128 * m:128 * m + 128].rearrange("(p o) -> p o", o=1)).then_inc(ld_ffn, 16)
            sp.wait_ge(ones_ok, 1)
            for u in range(2):
                rows = slice(64 * u + KS, 64 * u + 64)
                for t in (k_all, q_all):
                    for b in range(B):
                        sp.dma_start(t[rows, b], ones[:].unsqueeze(1).to_broadcast([16, C, HALF])).then_inc(fill_in, 16)
            for b in range(B):
                i = b % 2
                sp.wait_ge(q_split, 3 * b + 3)
                for part, t0, n in Q_REPS:
                    sp.dma_start(q_dram[b, :, t0:t0 + n],
                                 q_parts[:, i, part].unsqueeze(1).to_broadcast([128, n, T])).then_inc(q_out[b], 16)
                sp.wait_ge(v_nat_ok, b + 1)
                sp.dma_start(v_dram[b].rearrange("(t p) m -> p t m", p=128), v_nat[:, i]).then_inc(v_out[b], 16)
                sp.wait_ge(q_out[b], 16 * len(Q_REPS))
                for u in range(2):
                    src = q_dram[b].rearrange("(c d) t n -> (d t) c n", d=DK)[:, :, HALF * u:HALF * u + HALF]
                    sp.dma_start(q_all[half(u, KS), b], src).then_inc(qk_in[b], 16)
                sp.wait_ge(k_out[b], 16 * len(K_RUNS))
                for u in range(2):
                    src = k_dram[b].rearrange("(c d) t n -> (d t) c n", d=DK)[:, :, HALF * u:HALF * u + HALF]
                    sp.dma_start(k_all[half(u, KS), b], src).then_inc(qk_in[b], 16)
                sp.wait_ge(v_out[b], 16)
                for cl in range(4):
                    src = v_dram[b].rearrange("(h r) m -> r h m", r=R)[:, :, 32 * cl:32 * cl + 32]
                    sp.dma_start(v_all[32 * cl:32 * cl + 32, b], src).then_inc(v_in[b], 16)

            def rows_to_slot(q, count, b):
                sp.wait_ge(rows_ready, count)
                for cl in range(4):
                    sp.dma_start(m_dram[q, :, :, cl].rearrange("u k r -> k u r"),
                                 m_rows[32 * cl:32 * cl + MROWS, q]).then_inc(rows_out[q], 16)
                sp.wait_ge(rows_out[q], 64 * (b + 1))
                for u in range(2):
                    sp.dma_start(q_slot[64 * u + KS:64 * u + KM, q].rearrange("k p n -> k (p n)"),
                                 m_dram[q, u].rearrange("(k n) c r -> k (n c r)", k=3)).then_inc(rows_in[q], 16)

            def store(b, bi):
                sp.wait_ge(ln_done, 2 * b + 2)
                sp.dma_start(out[bi].rearrange("(t p) m -> p t m", p=128), x2[:, bi]).then_inc(stored, 16)

            def batch(b, first, last):
                for q in range(G):
                    if not (last and q == G - 1):
                        rows_to_slot((q + 1) % G, b * G + q + 2, b + (q + 1) // G)
                if not first:
                    store(b - 1, b - 1)

            rows_to_slot(0, 1, 0)
            batch(0, True, False)
            with sp.Fori(1, B - 1) as b:
                batch(b, False, False)
            batch(B - 1, False, True)
            store(B - 1, B - 1)
            sp.wait_ge(stored, 16 * B)

        @block.gpsimd
        def _(pool):
            pool.memset(one[:], 1.0).then_inc(consts_ok, 1)
            pool.memset(ident[:], 0.0).then_inc(ident_ok, 1)
            pool.wait_ge(ident_ok, 1)
            pool.affine_select(out=ident[:], in_=ident[:], compare_op=ALU.not_equal, fill=1.0, base=0,
                               pattern=[[-1, 128]], channel_multiplier=1).then_inc(ident_ok, 1)
            pool.memset(wo_pad[:], 0.0).then_inc(wo_pad_ok, 1)
            pool.wait_ge(ld_w, 64)
            pool.wait_ge(wo_pad_ok, 1)
            for o in range(2):
                for jb in range(2):
                    dst = wo_pad[:, o].rearrange("p (ja jb u e) -> p jb ja u e", jb=2, ja=2, u=2)[:, jb, :, :, 0:DK]
                    src = w_nat[:, 3].rearrange("p (jb o u ja d) -> p jb o ja u d", jb=2, o=2, u=2, ja=2)[:, jb, o]
                    pool.tensor_copy(dst, src).then_inc(wo_pad_ok, 1)
            pool.memset(den_sel[:], 0.0).then_inc(consts_ok, 1)
            pool.memset(m_src[:], 0.0).then_inc(consts_ok, 1)
            pool.memset(minus_half[:], -0.5).then_inc(consts_ok, 1)
            pool.wait_ge(consts_ok, 2)
            pool.affine_select(out=den_sel[:], in_=den_sel[:], compare_op=ALU.not_equal, fill=1.0, base=-DK,
                               pattern=[[-16, 8], [0, 16]], channel_multiplier=1).then_inc(consts_ok, 1)
            pool.memset(v_slot[:], 0.0).then_inc(v_zero, 1)
            pool.wait_ge(v_zero, 1)
            for q in range(G):
                c0 = 16 * (q % 2) + DK
                pool.memset(v_slot[:, q, :, :, c0:c0 + 1], 1.0).then_inc(v_zero, 1)

            for b in range(B):
                i = b % 2
                pool.wait_ge(kf_ok, 2 * b + 2)
                if b:
                    pool.wait_ge(k_split, 3 * b)
                pool.tensor_tensor(k_res[:], kf[:, i], k_parts[:, i, 0], ALU.subtract).then_inc(k_split, 1)
                pool.wait_ge(k_split, 3 * b + 1)
                pool.tensor_copy(k_parts[:, i, 1], k_res[:]).then_inc(k_split, 1)
                pool.wait_ge(k_split, 3 * b + 2)
                pool.tensor_tensor(k_parts[:, i, 2], k_res[:], k_parts[:, i, 1], ALU.subtract).then_inc(k_split, 1)
            pool.wait_ge(ld_small, 16 * n_small)
            for b in range(B):
                pool.wait_ge(ld_x[b], 16)
                pool.tensor_tensor(x_bo[:, b], x_nat[:, b], bias_bc[:, 1].unsqueeze(1).to_broadcast([128, TILES, D]),
                                   ALU.add).then_inc(x_bo_ok, 1)

            def copy_v(q, bi):
                c0 = 16 * (q % 2)
                for u in range(2):
                    dst = v_slot[:, q].rearrange("p (a u) k n -> p a u k n", u=2)[:, :, u, :, c0:c0 + DK]
                    src = v_all[:, bi, 8 * u + 2 * q:8 * u + 2 * q + 2].rearrange("p a (k d) -> p a k d", d=DK)
                    ins = pool.tensor_copy(dst, src)
                return ins

            def split_max(g, q):
                nm, r1 = neg_max[:, q], m_res[:]
                part = [m_src[:, :, 8 * i:8 * i + 8] for i in range(3)]
                pool.wait_ge(max_done, 16 * g + 16)
                pool.nop(nofuse=True)
                pool.tensor_copy(part[0], nm).then_inc(split_step, 1)
                pool.wait_ge(split_step, 4 * g + 1)
                pool.tensor_tensor(r1, nm, part[0], ALU.subtract).then_inc(split_step, 1)
                pool.wait_ge(split_step, 4 * g + 2)
                pool.nop(nofuse=True)
                pool.tensor_copy(part[1], r1).then_inc(split_step, 1)
                pool.wait_ge(split_step, 4 * g + 3)
                pool.tensor_tensor(part[2], r1, part[1], ALU.subtract).then_inc(split_step, 1)

            def copy_qk(q, bi):
                for slot, src in ((q_slot, q_all), (k_slot, k_all)):
                    for p in range(2):
                        rows = slice(2 * R * q + R * p, 2 * R * q + R * p + R)
                        ins = pool.tensor_copy(slot[:, q, p].rearrange("p (t c r) -> p t c r", t=4, c=4),
                                               src[:, bi, :, rows].rearrange("p (c t) r -> p t c r", c=4))
                return ins

            def refill(g, q, b):
                pool.wait_ge(st_ready, 8 * g + 8)
                pool.nop(nofuse=True)
                copy_qk(q, b + 1)
                pool.wait_ge(pv_done, 4 * g + 4)
                pool.nop(nofuse=True)
                copy_v(q, b + 1).then_inc(slot_step, 1)

            def normalize(oct_i, o):
                pool.wait_ge(rec_done, oct_i + 1)
                pool.tensor_tensor(y_norm[:, o], y_raw[:], y_rec[:], ALU.mult).then_inc(y_ready, 1)

            def inv_std(ln):
                pool.wait_ge(mv_done, ln + 1)
                pool.nop(nofuse=True)
                pool.tensor_scalar(var_eps[:], mv[:, :, 1], EPS, None, ALU.add).then_inc(var_done, 1)
                pool.wait_ge(var_done, ln + 1)
                pool.tensor_tensor(rstd[:], var_eps[:], minus_half[:], ALU.pow).then_inc(rstd_done, 1)

            def add_b2(ln):
                pool.wait_ge(ln_done, ln + 1)
                pool.tensor_tensor(x1_b2[:], x1[:], bias_bc[:, 2].unsqueeze(1).to_broadcast([128, TILES, D]),
                                   ALU.add).then_inc(x1b_done, 1)

            def batch(b, first, last):
                for q in range(G):
                    g = G * b + q
                    if q == 0 and not first:
                        normalize(2 * b - 1, 1)
                    if q == 1 and not first:
                        inv_std(2 * b - 2)
                        add_b2(2 * b - 2)
                    if q == 2:
                        normalize(2 * b, 0)
                    if not (last and q >= 2):
                        split_max(g + 2, (q + 2) % G)
                    if q == 3 and not first:
                        inv_std(2 * b - 1)
                    if not last:
                        refill(g, q, b)

            pool.wait_ge(v_in[0], 64)
            pool.wait_ge(v_zero, 1 + G)
            pool.wait_ge(qk_in[0], 64)
            pool.wait_ge(fill_in, 16 * 4 * B)
            for q in range(G):
                copy_qk(q, 0).then_inc(slots_first, 1)
            for q in range(G):
                ins = copy_v(q, 0)
            ins.then_inc(v_zero, 1)
            split_max(0, 0)
            split_max(1, 1)
            for b in range(1, B):
                pool.wait_ge(qk_in[b], 64)
                pool.wait_ge(v_in[b], 64)
            batch(0, True, False)
            with pool.Fori(1, B - 1) as b:
                batch(b, False, False)
            batch(B - 1, False, True)
            normalize(2 * B - 1, 1)
            inv_std(2 * B - 2)
            add_b2(2 * B - 2)
            inv_std(2 * B - 1)

        @block.scalar
        def _(act):
            for i, w in enumerate((wq, wk, wv, wo)):
                act.dma_start(w_nat[:, i], w).then_inc(ld_w, 16)
            for i, t in enumerate((rot_cos, rot_sin)):
                row = min(T, t.shape[0] - 1)
                act.dma_start(rot[:, i], t[row:row + 1]).then_inc(ld_small, 16)
            for i, t in enumerate((bq, bk)):
                act.dma_start(bqk[:, i:i + 1], t.rearrange("(p o) -> p o", o=1)).then_inc(ld_small, 16)

            def k_parts_out(b):
                act.wait_ge(k_split, 3 * b + 3)
                for t0, n in K_RUNS:
                    act.dma_start(k_dram[b, :, t0:t0 + n], k_parts[:, b % 2, 0:n]).then_inc(k_out[b], 16)

            act.wait_ge(wT_ps_ok, 1)
            act.copy(wT[:, 0:4].rearrange("p a m -> p (a m)"), st_ps[:, 0, 0]).then_inc(wT_ok, 1)
            act.wait_ge(wT_ps_ok, 2)
            act.copy(wT[:, 4], st_ps[:, 0, 1, 0:128]).then_inc(wT_ok, 1)
            for b in range(B):
                i = b % 2
                act.wait_ge(xT_ps_ok, b + 1)
                act.copy(xT[:, b], (o_ps if i else mi_ps)[:]).then_inc(xT_ok, 1)
                if b == 0:
                    act.wait_ge(g_ok, 2)
                if b >= 2:
                    act.wait_ge(q_split, 3 * b - 3)
                    act.wait_ge(q_out[b - 2], 48)
                    act.wait_ge(k_split, 3 * b - 3)
                    act.wait_ge(k_out[b - 2], 48)
                act.wait_ge(qk_ps_ok, 2 * b + 1)
                act.activation(qf[:, i], st_ps[:, 0, i], ACT.Identity, bias=bq_g[:], scale=g_col[:]).then_inc(qf_ok, 1)
                act.activation(q_parts[:, i, 0], st_ps[:, 0, i], ACT.Identity, bias=bq_g[:], scale=g_col[:]).then_inc(qf_ok, 1)
                act.wait_ge(qk_ps_ok, 2 * b + 2)
                act.activation(kf[:, i], st_ps[:, 1, i], ACT.Identity, bias=bqk[:, 1:2]).then_inc(kf_ok, 1)
                act.activation(k_parts[:, i, 0], st_ps[:, 1, i], ACT.Identity, bias=bqk[:, 1:2]).then_inc(kf_ok, 1)
                if b:
                    k_parts_out(b - 1)
            k_parts_out(B - 1)

            def group(g, q, b, first):
                for s in range(8):
                    kt, p = divmod(s, 2)
                    act.wait_ge(st_ready, 8 * g + s + 1)
                    if kt < 2:
                        if not (first and q == 0):
                            act.wait_ge(pv_done, 4 * g + kt - 1)
                    else:
                        act.wait_ge(pv_done, 4 * g + kt - 1)
                    act.activation(probs[:, kt % 2, p], st_ps[:, p], ACT.Exp).then_inc(exp_done, 1)
                    if s == 3 and q == 3 and not first:
                        act.wait_ge(hid_ready, 2 * b)
                        act.activation(hidT[:, 1], mi_ps[:], ACT.Relu, bias=b1_sb[:, 1:2]).then_inc(relu_done, 1)
                if q == 1 and not first:
                    copy_x1T(b)
                if q == 2 and not first:
                    act.wait_ge(hid_ready, 2 * b - 1)
                    act.activation(hidT[:, 0], mi_ps[:], ACT.Relu, bias=b1_sb[:, 0:1]).then_inc(relu_done, 1)
                if q % 2:
                    if not (first and q == 1):
                        act.wait_ge(y_ready, 2 * b + q // 2)
                    copy_o(2 * b + q // 2, 4 * g + 4)

            def copy_o(oct_i, count):
                act.wait_ge(pv_done, count)
                act.copy(y_raw[:].rearrange("p (r c t) -> p t c r", c=4, t=4), o_ps[:].rearrange("p (t c r) -> p t c r", c=4, t=4))\
                   .then_inc(o_copied, 1)

            def copy_x1T(b):
                act.wait_ge(x1T_ps_ok, b)
                act.copy(x1T[:], mi_ps[:]).then_inc(x1T_ok, 1)

            def batch(b, first):
                for q in range(G):
                    group(G * b + q, q, b, first)

            batch(0, True)
            with act.Fori(1, B) as b:
                batch(b, False)
            copy_x1T(B)
            for m in range(2):
                act.wait_ge(hid_ready, 2 * B - 1 + m)
                act.activation(hidT[:, m], mi_ps[:], ACT.Relu, bias=b1_sb[:, m:m + 1]).then_inc(relu_done, 1)

        @block.vector
        def _(dve):
            dve.memset(ones[:], 1.0).then_inc(ones_ok, 1)
            dve.wait_ge(ld_small, 16 * n_small)
            dve.tensor_tensor(rot_sq[:], rot[:], rot[:], ALU.mult).then_inc(rot_ok, 1)
            dve.wait_ge(rot_ok, 1)
            dve.tensor_tensor(rot_g[:], rot_sq[:, 0], rot_sq[:, 1], ALU.add).then_inc(rot_ok, 1)
            dve.wait_ge(rot_ok, 2)
            dve.tensor_scalar(g_row[:], rot_g[:].unsqueeze(1).unsqueeze(3).to_broadcast([1, C, DK // 2, 2]),
                              float(np.float32(1.0) / np.float32(np.sqrt(DK))), None, ALU.mult).then_inc(rot_ok, 1)
            dve.wait_ge(g_ps_ok, 1)
            dve.tensor_copy(g_col[:], mi_ps[:, 0:1]).then_inc(g_ok, 1)
            dve.wait_ge(g_ok, 1)
            dve.tensor_tensor(bq_g[:], bqk[:, 0:1], g_col[:], ALU.mult).then_inc(g_ok, 1)
            for b in range(B):
                i = b % 2
                dve.wait_ge(qf_ok, 2 * b + 2)
                if b:
                    dve.wait_ge(q_split, 3 * b)
                dve.tensor_tensor(q_res[:], qf[:, i], q_parts[:, i, 0], ALU.subtract).then_inc(q_split, 1)
                dve.wait_ge(q_split, 3 * b + 1)
                dve.tensor_copy(q_parts[:, i, 1], q_res[:]).then_inc(q_split, 1)
                dve.wait_ge(q_split, 3 * b + 2)
                dve.tensor_tensor(q_parts[:, i, 2], q_res[:], q_parts[:, i, 1], ALU.subtract).then_inc(q_split, 1)
                dve.wait_ge(v_ps_ok, b + 1)
                if b >= 2:
                    dve.wait_ge(v_out[b - 2], 16)
                dve.tensor_tensor(v_nat[:, i], s_ps[:, i].rearrange("p (t m) -> p t m", m=D),
                                  bias_bc[:, 0].unsqueeze(1).to_broadcast([128, TILES, D]), ALU.add).then_inc(v_nat_ok, 1)

            def maximum(g, q, m):
                p, qt, u = m // 8, m // 2 % 4, m % 2
                dve.wait_ge(scores_ready, 16 * g + m + 1)
                dve.tensor_reduce(neg_max[:, q, u, 4 * p + qt:4 * p + qt + 1], s_ps[:, m % 2], AX.X, ALU.max, negate=True)\
                   .then_inc(max_done, 1)

            def transpose_max(g, q):
                dve.wait_ge(split_step, 4 * g + 4)
                dve.transpose(m_rows[:, q].rearrange("p a r -> p (a r)"),
                              m_src[:].rearrange("p u k -> p (u k)")).then_inc(rows_ready, 1)

            def reciprocal(oct_i):
                dve.wait_ge(den_ready, oct_i + 1)
                dve.reciprocal(y_rec[:], mi_ps[:]).then_inc(rec_done, 1)

            def residual(ln, other):
                dve.tensor_tensor(res[:], mi_ps[:].rearrange("p (t m) -> p t m", m=D), other, ALU.add).then_inc(res_done, 1)
                dve.wait_ge(res_done, ln + 1)
                for t in range(TILES):
                    ins = dve.bn_stats(stats[:, t], res[:, t])
                ins.then_inc(stats_done, 1)
                dve.wait_ge(stats_done, ln + 1)
                dve.nop(nofuse=True)
                for t in range(TILES):
                    ins = dve.bn_aggr(mv[:, t], stats[:, t])
                ins.then_inc(mv_done, 1)

            def layernorm(ln, dst):
                dve.wait_ge(rstd_done, ln + 1)
                for t in range(TILES):
                    ins = dve.tensor_scalar(dst[:, t], res[:, t], mv[:, t, 0:1], rstd[:, t:t + 1], ALU.subtract, ALU.mult)
                ins.then_inc(ln_done, 1)

            def attn_residual(b, bi):
                dve.wait_ge(proj_ready, b + 1)
                residual(2 * b, x_bo[:, bi])

            def ffn_residual(b):
                dve.wait_ge(x1b_done, b + 1)
                dve.wait_ge(y2_ready, b + 1)
                residual(2 * b + 1, x1_b2[:])

            def batch(b, first, last):
                for q in range(G):
                    g = G * b + q
                    for m in range(16):
                        if m == 3 and not (last and q == G - 1):
                            transpose_max(g + 1, (q + 1) % G)
                        if m == 6 and q == 0 and not first:
                            reciprocal(2 * b - 1)
                        if m == 6 and q == 1 and not first:
                            attn_residual(b - 1, b - 1)
                        if m == 11 and q == 1 and not first:
                            layernorm(2 * b - 2, x1[:])
                        if m == 6 and q == 2:
                            reciprocal(2 * b)
                        if not (last and q >= 2):
                            maximum(g + 2, (q + 2) % G, m)
                if not first:
                    ffn_residual(b - 1)
                    layernorm(2 * b - 1, x2[:, b - 1])

            for m in range(16):
                maximum(0, 0, m)
            transpose_max(0, 0)
            for m in range(16):
                maximum(1, 1, m)
            dve.wait_ge(x_bo_ok, B)
            batch(0, True, False)
            with dve.Fori(1, B - 1) as b:
                batch(b, False, False)
            batch(B - 1, False, True)
            reciprocal(2 * B - 1)
            attn_residual(B - 1, B - 1)
            layernorm(2 * B - 2, x1[:])
            ffn_residual(B - 1)
            layernorm(2 * B - 1, x2[:, B - 1])

        @block.tensor
        def _(pe):
            pe.wait_ge(ident_ok, 2)
            pe.wait_ge(consts_ok, 1)
            pe.wait_ge(ld_w, 64)
            for i in range(3):
                pe.transpose(st_ps[:, 0, 0, 128 * i:128 * i + 128], w_nat[:, i], ident[:])
            pe.wait_ge(wo_pad_ok, 5)
            pe.transpose(st_ps[:, 0, 0, 384:512], wo_pad[:, 0], ident[:]).then_inc(wT_ps_ok, 1)
            pe.transpose(st_ps[:, 0, 1, 0:128], wo_pad[:, 1], ident[:]).then_inc(wT_ps_ok, 1)
            pe.wait_ge(rot_ok, 3)
            pe.matmul(mi_ps[:, 0:1], g_row[:].rearrange("o c j i -> o (c j i)"), one[:], start=True, stop=True).then_inc(g_ps_ok, 1)
            pe.wait_ge(g_ok, 1)
            for b in range(B):
                i = b % 2
                xb = o_ps if i else mi_ps
                pe.wait_ge(ld_x[b], 16)
                for t in range(TILES):
                    ins = pe.transpose(xb[:, 128 * t:128 * t + 128], x_nat[:, b, t], ident[:])
                ins.then_inc(xT_ps_ok, 1)
                pe.wait_ge(xT_ok, b + 1)
                if b == 0:
                    pe.wait_ge(wT_ok, 2)
                if b >= 2:
                    pe.wait_ge(qf_ok, 2 * b - 2)
                    pe.wait_ge(kf_ok, 2 * b - 2)
                    pe.wait_ge(v_nat_ok, b - 1)
                pe.matmul(st_ps[:, 0, i], wT[:, 0], xT[:, b], start=True, stop=True).then_inc(qk_ps_ok, 1)
                pe.matmul(st_ps[:, 1, i], wT[:, 1], xT[:, b], start=True, stop=True).then_inc(qk_ps_ok, 1)
                for t in range(TILES):
                    ins = pe.matmul(s_ps[:, i, 128 * t:128 * t + 128], xT[:, b, 128 * t:128 * t + 128], wT[:, 2],
                                    start=True, stop=True)
                ins.then_inc(v_ps_ok, 1)
            pe.wait_ge(qf_ok, 2 * B)
            pe.wait_ge(kf_ok, 2 * B)
            pe.wait_ge(v_nat_ok, B)

            def score(g, q, m, free):
                p, qt, u = m // 8, m // 2 % 4, m % 2
                if free:
                    pe.wait_ge(max_done, 16 * g + m - 1)
                rows = half(u, KS)
                pe.matmul(s_ps[:, m % 2], q_slot[rows, q, p, 128 * qt:128 * qt + 128], k_slot[rows, q, p],
                          start=True, stop=True).then_inc(scores_ready, 1)

            def score_t(g, q, s, free):
                kt, p = divmod(s, 2)
                if free:
                    pe.wait_ge(exp_done, 8 * g + s - 1)
                for u in range(2):
                    rows = half(u, KM)
                    ins = pe.matmul(st_ps[:, p, u], k_slot[rows, q, p, 128 * kt:128 * kt + 128], q_slot[rows, q, p],
                                    start=True, stop=True)
                ins.then_inc(st_ready, 1)

            def values(g, q, kt):
                pe.wait_ge(exp_done, 8 * g + 2 * kt + 2)
                for j in range(4):
                    ins = pe.matmul(o_ps[32 * j:32 * j + 32], v_slot[:, q, j, kt], probs[:, kt % 2, j // 2, j % 2],
                                    start=(q % 2 == 0 and kt == 0), stop=(q % 2 == 1 and kt == 3))
                ins.then_inc(pv_done, 1)

            def denominators(oct_i):
                pe.wait_ge(o_copied, oct_i + 1)
                pe.matmul(mi_ps[:], den_sel[:], y_raw[:], start=True, stop=True).then_inc(den_ready, 1)

            def project(b):
                pe.wait_ge(y_ready, 2 * b + 2)
                for t in range(TILES):
                    for o in range(2):
                        ins = pe.matmul(mi_ps[:, 128 * t:128 * t + 128], y_norm[:, o, 128 * t:128 * t + 128], wT[:, 3 + o],
                                        start=(o == 0), stop=(o == 1))
                ins.then_inc(proj_ready, 1)

            def transpose_x1(b):
                pe.wait_ge(ln_done, 2 * b + 1)
                for t in range(TILES):
                    ins = pe.transpose(mi_ps[:, 128 * t:128 * t + 128], x1[:, t], ident[:])
                ins.then_inc(x1T_ps_ok, 1)

            def hidden(b, m):
                pe.wait_ge(x1T_ok, b + 1)
                if m:
                    pe.wait_ge(relu_done, 2 * b + 1)
                pe.matmul(mi_ps[:], w1_sb[:, 128 * m:128 * m + 128], x1T[:], start=True, stop=True).then_inc(hid_ready, 1)

            def ffn_out(b):
                pe.wait_ge(relu_done, 2 * b + 2)
                for t in range(TILES):
                    for m in range(2):
                        ins = pe.matmul(mi_ps[:, 128 * t:128 * t + 128], hidT[:, m, 128 * t:128 * t + 128], w2_sb[:, m],
                                        start=(m == 0), stop=(m == 1))
                ins.then_inc(y2_ready, 1)

            def batch(b, first, last):
                for q in range(G):
                    g = G * b + q
                    if not (last and q >= 2):
                        if first and q < 2:
                            pe.wait_ge(slots_first, g + 3)
                        else:
                            pe.wait_ge(slot_step, g - 1)
                    pe.wait_ge(rows_in[q], 32 * (b + 1))
                    for kt in range(4):
                        for p in range(2):
                            s = 2 * kt + p
                            score_t(g, q, s, not (first and q == 0 and s < 2))
                            if not (last and q >= 2):
                                for m in range(2):
                                    score(g + 2, (q + 2) % G, 2 * s + m, True)
                        if kt == 1:
                            if q % 2 == 0 and not (first and q == 0):
                                pe.wait_ge(o_copied, 2 * b + q // 2)
                        if kt:
                            values(g, q, kt - 1)
                        if (q, kt) == (0, 1) and not first:
                            denominators(2 * b - 1)
                        if (q, kt) == (1, 1) and not first:
                            project(b - 1)
                        if (q, kt) == (1, 3) and not first:
                            transpose_x1(b - 1)
                        if (q, kt) == (2, 1):
                            if not first:
                                pe.wait_ge(x1T_ok, b)
                            denominators(2 * b)
                        if (q, kt) == (2, 3) and not first:
                            pe.wait_ge(rec_done, 2 * b + 1)
                            hidden(b - 1, 0)
                        if (q, kt) == (3, 1) and not first:
                            hidden(b - 1, 1)
                        if (q, kt) == (3, 3) and not first:
                            ffn_out(b - 1)
                    values(g, q, 3)

            for g in range(2):
                pe.wait_ge(slots_first, g + 1)
                for m in range(16):
                    score(g, g, m, not (g == 0 and m < 2))
            pe.wait_ge(v_zero, 2 + G)
            pe.wait_ge(ld_ffn, 64)
            pe.wait_ge(consts_ok, 5)
            batch(0, True, False)
            with pe.Fori(1, B - 1) as b:
                batch(b, False, False)
            batch(B - 1, False, True)
            pe.wait_ge(res_done, 2 * B - 2)
            denominators(2 * B - 1)
            project(B - 1)
            transpose_x1(B - 1)
            hidden(B - 1, 0)
            hidden(B - 1, 1)
            ffn_out(B - 1)


_INS = ["L0_attn_x", "L0_attn_wq", "L0_attn_bq", "L0_attn_wk", "L0_attn_bk", "L0_attn_wv", "L0_attn_bv", "L0_attn_wo",
        "L0_attn_bo", "L0_attn_rot_cos", "L0_attn_rot_sin", "L0_ffn_W1", "L0_ffn_b1", "L0_ffn_W2", "L0_ffn_b2"]


def kernel(**inputs):
    import numpy as _np
    import concourse.bacc as _bacc
    from concourse import mybir as _mybir
    from concourse.bass_utils import run_bass_kernel_spmd as _run

    nc = _bacc.Bacc("TRN2", target_bir_lowering=False, num_devices=1)
    arrays, args = {}, []
    for name in _INS:
        a = _np.ascontiguousarray(inputs[name])
        arrays[f"in_{name}"] = a
        args.append(nc.dram_tensor(f"in_{name}", a.shape, _mybir.dt.from_np(a.dtype), kind="ExternalInput").ap())
    args.append(nc.dram_tensor("out_0", (B, T, D), _mybir.dt.float32, kind="ExternalOutput").ap())
    build_layer(nc, *args)
    r = _run(nc, [arrays], core_ids=[0])
    return r.results[0]["out_0"]
```

```python
from contextlib import ExitStack

import numpy as np

import concourse.bass as bass
from concourse import mybir

F32 = mybir.dt.float32
BF16 = mybir.dt.bfloat16
ALU = mybir.AluOpType
ACT = mybir.ActivationFunctionType
AX = mybir.AxisListType

B, T, D = 4, 512, 128
H, DK = 16, 8
E_SEL, HID = 1, 256
R, C = T // H, D // DK
TILES = T // 128
G = 4
N = B * G
HALF = T // 2
TERMS = 6
KS = TERMS * DK
KM = KS + 3
MROWS = 24
EPS = 1e-5


def half(u, rows):
    return slice(64 * u, 64 * u + rows)


def build_layer(nc, x, wq, bq, wk, bk, wv, bv, wo, bo, rot_cos, rot_sin, w1, b1, w2, b2, out):
    with ExitStack() as ctx:
        def sb(name, shape, dt=F32):
            return ctx.enter_context(nc.sbuf_tensor(name, shape, dt))

        def ps(name, shape, dt=F32):
            return ctx.enter_context(nc.psum_tensor(name, shape, dt))

        def sem(name):
            return ctx.enter_context(nc.semaphore(name))

        q_dram = nc.dram_tensor("q_dram", (B, 128, TERMS, T), BF16, kind="Internal").ap()
        k_dram = nc.dram_tensor("k_dram", (B, 128, TERMS, T), BF16, kind="Internal").ap()
        v_dram = nc.dram_tensor("v_dram", (B, T, D), F32, kind="Internal").ap()
        m_dram = nc.dram_tensor("m_dram", (G, 2, MROWS, 4, R), BF16, kind="Internal").ap()

        x_nat = sb("x_nat", [128, B, TILES, D])
        x_bo = sb("x_bo", [128, B, TILES, D])
        xT = sb("xT", [128, B, T])
        w_nat = sb("w_nat", [128, 4, 128])
        wo_perm = sb("wo_perm", [128, 128])
        wT = sb("wT", [128, 4, 128])
        w1_sb = sb("w1_sb", [128, HID])
        w2_sb = sb("w2_sb", [128, 2, D])
        b1_sb = sb("b1_sb", [128, 2])
        bias_bc = sb("bias_bc", [128, 3, D])
        bqk = sb("bqk", [128, 2])
        rot = sb("rot", [1, 2, DK // 2])
        rot_sq = sb("rot_sq", [1, 2, DK // 2])
        rot_g = sb("rot_g", [1, DK // 2])
        g_row = sb("g_row", [1, C, DK // 2, 2])
        g_col = sb("g_col", [128, 1])
        bq_g = sb("bq_g", [128, 1])
        one = sb("one", [1, 1])
        ident = sb("ident", [128, 128])
        ones = sb("ones", [16, HALF], BF16)
        qf = sb("qf", [128, 2, T])
        kf = sb("kf", [128, 2, T])
        q_res = sb("q_res", [128, T])
        k_res = sb("k_res", [128, T])
        q_parts = sb("q_parts", [128, 2, 3, T], BF16)
        k_parts = sb("k_parts", [128, 2, 3, T], BF16)
        v_nat = sb("v_nat", [128, 2, TILES, D])
        q_all = sb("q_all", [128, B, C, HALF], BF16)
        k_all = sb("k_all", [128, B, C, HALF], BF16)
        q_slot = sb("q_slot", [128, G, 2, T], BF16)
        k_slot = sb("k_slot", [128, G, 2, T], BF16)
        v_all = sb("v_all", [128, B, H, 4 * DK])
        v_slot = sb("v_slot", [128, G, 4, 4, 32])
        neg_max = sb("neg_max", [128, G, 2, 8])
        m_res = sb("m_res", [128, 2, 8])
        m_src = sb("m_src", [128, 2, 32], BF16)
        m_rows = sb("m_rows", [128, G, 2, 32], BF16)
        probs = sb("probs", [128, 2, 2, 2, T])
        y_raw = sb("y_raw", [128, T])
        y_rec = sb("y_rec", [128, TILES, 8])
        attn = sb("attn", [128, TILES, 2, 8, DK])
        attnT = sb("attnT", [128, T])
        res = sb("res", [128, TILES, D])
        stats = sb("stats", [128, TILES, 6])
        mv = sb("mv", [128, TILES, 2])
        var_eps = sb("var_eps", [128, TILES])
        minus_half = sb("minus_half", [128, TILES])
        rstd = sb("rstd", [128, TILES])
        x1 = sb("x1", [128, TILES, D])
        x1_b2 = sb("x1_b2", [128, TILES, D])
        x1T = sb("x1T", [128, T])
        hidT = sb("hidT", [128, 2, T])
        x2 = sb("x2", [128, B, TILES, D])

        st_ps = ps("st_ps", [128, 2, 2, T])
        s_ps = ps("s_ps", [128, 2, T])
        o_ps = ps("o_ps", [128, T])
        mi_ps = ps("mi_ps", [128, T])

        ld_w = sem("ld_w")
        ld_small = sem("ld_small")
        ld_x = [sem(f"ld_x{b}") for b in range(B)]
        ld_ffn = sem("ld_ffn")
        ident_ok = sem("ident_ok")
        consts_ok = sem("consts_ok")
        rot_ok = sem("rot_ok")
        g_ps_ok = sem("g_ps_ok")
        g_ok = sem("g_ok")
        wT_ps_ok = sem("wT_ps_ok")
        wT_ok = sem("wT_ok")
        wo_ok = sem("wo_ok")
        xT_ps_ok = sem("xT_ps_ok")
        xT_ok = sem("xT_ok")
        qk_ps_ok = sem("qk_ps_ok")
        v_ps_ok = sem("v_ps_ok")
        qf_ok = sem("qf_ok")
        kf_ok = sem("kf_ok")
        v_nat_ok = sem("v_nat_ok")
        q_split = sem("q_split")
        k_split = sem("k_split")
        q_out = [sem(f"q_out{b}") for b in range(B)]
        k_out = [sem(f"k_out{b}") for b in range(B)]
        v_out = [sem(f"v_out{b}") for b in range(B)]
        qk_in = [sem(f"qk_in{b}") for b in range(B)]
        v_in = [sem(f"v_in{b}") for b in range(B)]
        ones_ok = sem("ones_ok")
        fill_in = sem("fill_in")
        x_bo_ok = sem("x_bo_ok")
        v_zero = sem("v_zero")
        scores_ready = sem("scores_ready")
        max_done = sem("max_done")
        split_step = sem("split_step")
        rows_ready = sem("rows_ready")
        rows_out = [sem(f"rows_out{q}") for q in range(G)]
        rows_in = [sem(f"rows_in{q}") for q in range(G)]
        st_ready = sem("st_ready")
        exp_done = sem("exp_done")
        pv_done = sem("pv_done")
        o_copied = sem("o_copied")
        yT_ready = sem("yT_ready")
        rec_done = sem("rec_done")
        norm_done = sem("norm_done")
        aT_ps_ok = sem("aT_ps_ok")
        aT_ok = sem("aT_ok")
        slots_first = sem("slots_first")
        slot_step = sem("slot_step")
        proj_ready = sem("proj_ready")
        res_done = sem("res_done")
        stats_done = sem("stats_done")
        mv_done = sem("mv_done")
        var_done = sem("var_done")
        rstd_done = sem("rstd_done")
        ln_done = sem("ln_done")
        x1b_done = sem("x1b_done")
        x1T_ps_ok = sem("x1T_ps_ok")
        x1T_ok = sem("x1T_ok")
        hid_ready = sem("hid_ready")
        relu_done = sem("relu_done")
        y2_ready = sem("y2_ready")
        stored = sem("stored")

        block = ctx.enter_context(nc.Block())
        Q_REPS = ((0, 0, 3), (1, 3, 2), (2, 5, 1))
        K_RUNS = ((0, 3), (3, 2), (5, 1))
        n_small = 2 + 2 + 3

        def slot_and_source(slot, src, q, p, bi):
            rows = slice(2 * R * q + R * p, 2 * R * q + R * p + R)
            return (slot[:, q, p].rearrange("p (t c r) -> p t c r", t=4, c=4),
                    src[:, bi, :, rows].rearrange("p (c t) r -> p t c r", c=4))

        @block.sync
        def _(sp):
            for b in range(B):
                sp.dma_start(x_nat[:, b], x[b].rearrange("(t p) m -> p t m", p=128)).then_inc(ld_x[b], 16)
            for i, w in enumerate((bv, bo, b2[E_SEL])):
                sp.dma_start(bias_bc[:, i], w.partition_broadcast(128)).then_inc(ld_small, 16)
            sp.dma_start(w1_sb[:], w1[E_SEL]).then_inc(ld_ffn, 16)
            sp.dma_start(w2_sb[:], w2[E_SEL].rearrange("(m p) n -> p m n", p=128)).then_inc(ld_ffn, 16)
            for m in range(2):
                sp.dma_start(b1_sb[:, m:m + 1], b1[E_SEL, 128 * m:128 * m + 128].rearrange("(p o) -> p o", o=1)).then_inc(ld_ffn, 16)
            sp.wait_ge(ones_ok, 1)
            for u in range(2):
                rows = slice(64 * u + KS, 64 * u + 64)
                for t in (k_all, q_all):
                    for b in range(B):
                        sp.dma_start(t[rows, b], ones[:].unsqueeze(1).to_broadcast([16, C, HALF])).then_inc(fill_in, 16)
            for b in range(B):
                i = b % 2
                sp.wait_ge(q_split, 3 * b + 3)
                for part, t0, n in Q_REPS:
                    sp.dma_start(q_dram[b, :, t0:t0 + n],
                                 q_parts[:, i, part].unsqueeze(1).to_broadcast([128, n, T])).then_inc(q_out[b], 16)
                sp.wait_ge(v_nat_ok, b + 1)
                sp.dma_start(v_dram[b].rearrange("(t p) m -> p t m", p=128), v_nat[:, i]).then_inc(v_out[b], 16)
                sp.wait_ge(q_out[b], 16 * len(Q_REPS))
                for u in range(2):
                    src = q_dram[b].rearrange("(c d) t n -> (d t) c n", d=DK)[:, :, HALF * u:HALF * u + HALF]
                    sp.dma_start(q_all[half(u, KS), b], src).then_inc(qk_in[b], 16)
                sp.wait_ge(k_out[b], 16 * len(K_RUNS))
                for u in range(2):
                    src = k_dram[b].rearrange("(c d) t n -> (d t) c n", d=DK)[:, :, HALF * u:HALF * u + HALF]
                    sp.dma_start(k_all[half(u, KS), b], src).then_inc(qk_in[b], 16)
                sp.wait_ge(v_out[b], 16)
                for cl in range(4):
                    src = v_dram[b].rearrange("(h r) m -> r h m", r=R)[:, :, 32 * cl:32 * cl + 32]
                    sp.dma_start(v_all[32 * cl:32 * cl + 32, b], src).then_inc(v_in[b], 16)

            def rows_to_slot(q, count, b):
                sp.wait_ge(rows_ready, count)
                for cl in range(4):
                    sp.dma_start(m_dram[q, :, :, cl].rearrange("u k r -> k u r"),
                                 m_rows[32 * cl:32 * cl + MROWS, q]).then_inc(rows_out[q], 16)
                sp.wait_ge(rows_out[q], 64 * (b + 1))
                for u in range(2):
                    sp.dma_start(q_slot[64 * u + KS:64 * u + KM, q].rearrange("k p n -> k (p n)"),
                                 m_dram[q, u].rearrange("(k n) c r -> k (n c r)", k=3)).then_inc(rows_in[q], 16)

            def store(b, bi):
                sp.wait_ge(ln_done, 2 * b + 2)
                sp.dma_start(out[bi].rearrange("(t p) m -> p t m", p=128), x2[:, bi]).then_inc(stored, 16)

            def batch(b, first, last):
                for q in range(G):
                    if not (last and q == G - 1):
                        rows_to_slot((q + 1) % G, b * G + q + 2, b + (q + 1) // G)
                if not first:
                    store(b - 1, b - 1)

            rows_to_slot(0, 1, 0)
            batch(0, True, False)
            with sp.Fori(1, B - 1) as b:
                batch(b, False, False)
            batch(B - 1, False, True)
            store(B - 1, B - 1)
            sp.wait_ge(stored, 16 * B)

        @block.gpsimd
        def _(pool):
            pool.memset(one[:], 1.0).then_inc(consts_ok, 1)
            pool.memset(ident[:], 0.0).then_inc(ident_ok, 1)
            pool.wait_ge(ident_ok, 1)
            pool.affine_select(out=ident[:], in_=ident[:], compare_op=ALU.not_equal, fill=1.0, base=0,
                               pattern=[[-1, 128]], channel_multiplier=1).then_inc(ident_ok, 1)
            pool.wait_ge(ld_w, 64)
            for o in range(2):
                for jb in range(2):
                    dst = wo_perm[:].rearrange("p (o ja jb u d) -> p o jb ja u d", o=2, ja=2, jb=2, u=2)[:, o, jb]
                    src = w_nat[:, 3].rearrange("p (jb o u ja d) -> p o jb ja u d", jb=2, o=2, u=2, ja=2)[:, o, jb]
                    pool.tensor_copy(dst, src).then_inc(wo_ok, 1)
            pool.memset(m_src[:], 0.0).then_inc(consts_ok, 1)
            pool.memset(minus_half[:], -0.5).then_inc(consts_ok, 1)
            pool.memset(v_slot[:], 0.0).then_inc(v_zero, 1)
            pool.wait_ge(v_zero, 1)
            for q in range(G):
                c0 = 16 * (q % 2) + DK
                pool.memset(v_slot[:, q, :, :, c0:c0 + 1], 1.0).then_inc(v_zero, 1)

            for b in range(B):
                i = b % 2
                pool.wait_ge(kf_ok, 2 * b + 2)
                if b:
                    pool.wait_ge(k_split, 3 * b)
                pool.tensor_tensor(k_res[:], kf[:, i], k_parts[:, i, 0], ALU.subtract).then_inc(k_split, 1)
                pool.wait_ge(k_split, 3 * b + 1)
                pool.tensor_copy(k_parts[:, i, 1], k_res[:]).then_inc(k_split, 1)
                pool.wait_ge(k_split, 3 * b + 2)
                pool.tensor_tensor(k_parts[:, i, 2], k_res[:], k_parts[:, i, 1], ALU.subtract).then_inc(k_split, 1)
            pool.wait_ge(ld_small, 16 * n_small)
            for b in range(B):
                pool.wait_ge(ld_x[b], 16)
                pool.tensor_tensor(x_bo[:, b], x_nat[:, b], bias_bc[:, 1].unsqueeze(1).to_broadcast([128, TILES, D]),
                                   ALU.add).then_inc(x_bo_ok, 1)

            def copy_v(q, bi):
                c0 = 16 * (q % 2)
                for u in range(2):
                    dst = v_slot[:, q].rearrange("p (a u) k n -> p a u k n", u=2)[:, :, u, :, c0:c0 + DK]
                    src = v_all[:, bi, 8 * u + 2 * q:8 * u + 2 * q + 2].rearrange("p a (k d) -> p a k d", d=DK)
                    ins = pool.tensor_copy(dst, src)
                return ins

            def split_max(g, q):
                nm, r1 = neg_max[:, q], m_res[:]
                part = [m_src[:, :, 8 * i:8 * i + 8] for i in range(3)]
                pool.wait_ge(max_done, 16 * g + 16)
                pool.nop(nofuse=True)
                pool.tensor_copy(part[0], nm).then_inc(split_step, 1)
                pool.wait_ge(split_step, 4 * g + 1)
                pool.tensor_tensor(r1, nm, part[0], ALU.subtract).then_inc(split_step, 1)
                pool.wait_ge(split_step, 4 * g + 2)
                pool.nop(nofuse=True)
                pool.tensor_copy(part[1], r1).then_inc(split_step, 1)
                pool.wait_ge(split_step, 4 * g + 3)
                pool.tensor_tensor(part[2], r1, part[1], ALU.subtract).then_inc(split_step, 1)

            def copy_qk(q, bi):
                for slot, src in ((q_slot, q_all), (k_slot, k_all)):
                    for p in range(2):
                        ins = pool.tensor_copy(*slot_and_source(slot, src, q, p, bi))
                return ins

            def refill(g, q, b):
                pool.wait_ge(st_ready, 8 * g + 8)
                pool.nop(nofuse=True)
                copy_qk(q, b + 1)
                pool.wait_ge(pv_done, 4 * g + 4)
                pool.nop(nofuse=True)
                copy_v(q, b + 1).then_inc(slot_step, 1)

            def inv_std(ln):
                pool.wait_ge(mv_done, ln + 1)
                pool.nop(nofuse=True)
                pool.tensor_scalar(var_eps[:], mv[:, :, 1], EPS, None, ALU.add).then_inc(var_done, 1)
                pool.wait_ge(var_done, ln + 1)
                pool.tensor_tensor(rstd[:], var_eps[:], minus_half[:], ALU.pow).then_inc(rstd_done, 1)

            def add_b2(ln):
                pool.wait_ge(ln_done, ln + 1)
                pool.tensor_tensor(x1_b2[:], x1[:], bias_bc[:, 2].unsqueeze(1).to_broadcast([128, TILES, D]),
                                   ALU.add).then_inc(x1b_done, 1)

            def batch(b, first, last):
                for q in range(G):
                    g = G * b + q
                    if q == 1 and not first:
                        inv_std(2 * b - 2)
                    if not (last and q >= 2):
                        split_max(g + 2, (q + 2) % G)
                    if q == 1 and not first:
                        add_b2(2 * b - 2)
                    if q == 3 and not first:
                        inv_std(2 * b - 1)
                    if not last:
                        refill(g, q, b)

            pool.wait_ge(v_in[0], 64)
            pool.wait_ge(v_zero, 1 + G)
            for q in range(G):
                ins = copy_v(q, 0)
            ins.then_inc(v_zero, 1)
            split_max(0, 0)
            split_max(1, 1)
            for b in range(1, B):
                pool.wait_ge(qk_in[b], 64)
                pool.wait_ge(v_in[b], 64)
            batch(0, True, False)
            with pool.Fori(1, B - 1) as b:
                batch(b, False, False)
            batch(B - 1, False, True)
            inv_std(2 * B - 2)
            add_b2(2 * B - 2)
            inv_std(2 * B - 1)

        @block.scalar
        def _(act):
            for i, w in enumerate((wq, wk, wv, wo)):
                act.dma_start(w_nat[:, i], w).then_inc(ld_w, 16)
            for i, t in enumerate((rot_cos, rot_sin)):
                row = min(T, t.shape[0] - 1)
                act.dma_start(rot[:, i], t[row:row + 1]).then_inc(ld_small, 16)
            for i, t in enumerate((bq, bk)):
                act.dma_start(bqk[:, i:i + 1], t.rearrange("(p o) -> p o", o=1)).then_inc(ld_small, 16)

            def k_parts_out(b):
                act.wait_ge(k_split, 3 * b + 3)
                for t0, n in K_RUNS:
                    act.dma_start(k_dram[b, :, t0:t0 + n], k_parts[:, b % 2, 0:n]).then_inc(k_out[b], 16)

            act.wait_ge(wT_ps_ok, 1)
            act.copy(wT[:].rearrange("p a m -> p (a m)"), st_ps[:, 0, 0]).then_inc(wT_ok, 1)
            for b in range(B):
                i = b % 2
                act.wait_ge(xT_ps_ok, b + 1)
                act.copy(xT[:, b], (o_ps if i else mi_ps)[:]).then_inc(xT_ok, 1)
                if b == 0:
                    act.wait_ge(g_ok, 2)
                if b >= 2:
                    act.wait_ge(q_split, 3 * b - 3)
                    act.wait_ge(q_out[b - 2], 48)
                    act.wait_ge(k_split, 3 * b - 3)
                    act.wait_ge(k_out[b - 2], 48)
                act.wait_ge(qk_ps_ok, 2 * b + 1)
                act.activation(qf[:, i], st_ps[:, 0, i], ACT.Identity, bias=bq_g[:], scale=g_col[:]).then_inc(qf_ok, 1)
                act.activation(q_parts[:, i, 0], st_ps[:, 0, i], ACT.Identity, bias=bq_g[:], scale=g_col[:]).then_inc(qf_ok, 1)
                act.wait_ge(qk_ps_ok, 2 * b + 2)
                act.activation(kf[:, i], st_ps[:, 1, i], ACT.Identity, bias=bqk[:, 1:2]).then_inc(kf_ok, 1)
                act.activation(k_parts[:, i, 0], st_ps[:, 1, i], ACT.Identity, bias=bqk[:, 1:2]).then_inc(kf_ok, 1)
                if b:
                    k_parts_out(b - 1)
            k_parts_out(B - 1)

            def group(g, q, b, first):
                for s in range(8):
                    kt, p = divmod(s, 2)
                    act.wait_ge(st_ready, 8 * g + s + 1)
                    if kt < 2:
                        if not (first and q == 0):
                            act.wait_ge(pv_done, 4 * g + kt - 1)
                    else:
                        act.wait_ge(pv_done, 4 * g + kt - 1)
                    act.activation(probs[:, kt % 2, p], st_ps[:, p], ACT.Exp).then_inc(exp_done, 1)
                    if s == 1 and q == 1 and not first:
                        copy_aT(b - 1)
                    if s == 1 and q == 2 and not first:
                        copy_x1T(b - 1)
                    if s == 2 and q % 2 == 0 and not (first and q == 0):
                        copy_o(2 * b + q // 2 - 1, 4 * g, first)
                    if s == 3 and q == 3 and not first:
                        relu(b - 1, 1)
                if q == 2 and not first:
                    relu(b - 1, 0)

            def copy_o(oct_i, count, first):
                act.wait_ge(pv_done, count)
                if not first:
                    act.wait_ge(yT_ready, oct_i)
                act.copy(y_raw[:].rearrange("p (r c t) -> p t c r", c=4, t=4), o_ps[:].rearrange("p (t c r) -> p t c r", c=4, t=4))\
                   .then_inc(o_copied, 1)

            def copy_aT(b):
                act.wait_ge(aT_ps_ok, b + 1)
                act.copy(attnT[:], mi_ps[:]).then_inc(aT_ok, 1)

            def copy_x1T(b):
                act.wait_ge(x1T_ps_ok, b + 1)
                act.copy(x1T[:], mi_ps[:]).then_inc(x1T_ok, 1)

            def relu(b, m):
                act.wait_ge(hid_ready, 2 * b + m + 1)
                act.activation(hidT[:, m], mi_ps[:], ACT.Relu, bias=b1_sb[:, m:m + 1]).then_inc(relu_done, 1)

            def batch(b, first):
                for q in range(G):
                    group(G * b + q, q, b, first)

            batch(0, True)
            with act.Fori(1, B) as b:
                batch(b, False)
            copy_o(2 * B - 1, 4 * N, False)
            copy_aT(B - 1)
            copy_x1T(B - 1)
            for m in range(2):
                relu(B - 1, m)

        @block.vector
        def _(dve):
            dve.memset(ones[:], 1.0).then_inc(ones_ok, 1)
            dve.wait_ge(ld_small, 16 * n_small)
            dve.tensor_tensor(rot_sq[:], rot[:], rot[:], ALU.mult).then_inc(rot_ok, 1)
            dve.wait_ge(rot_ok, 1)
            dve.tensor_tensor(rot_g[:], rot_sq[:, 0], rot_sq[:, 1], ALU.add).then_inc(rot_ok, 1)
            dve.wait_ge(rot_ok, 2)
            dve.tensor_scalar(g_row[:], rot_g[:].unsqueeze(1).unsqueeze(3).to_broadcast([1, C, DK // 2, 2]),
                              float(np.float32(1.0) / np.float32(np.sqrt(DK))), None, ALU.mult).then_inc(rot_ok, 1)
            dve.wait_ge(g_ps_ok, 1)
            dve.tensor_copy(g_col[:], mi_ps[:, 0:1]).then_inc(g_ok, 1)
            dve.wait_ge(g_ok, 1)
            dve.tensor_tensor(bq_g[:], bqk[:, 0:1], g_col[:], ALU.mult).then_inc(g_ok, 1)
            for b in range(B):
                i = b % 2
                dve.wait_ge(qf_ok, 2 * b + 2)
                if b:
                    dve.wait_ge(q_split, 3 * b)
                dve.tensor_tensor(q_res[:], qf[:, i], q_parts[:, i, 0], ALU.subtract).then_inc(q_split, 1)
                dve.wait_ge(q_split, 3 * b + 1)
                dve.tensor_copy(q_parts[:, i, 1], q_res[:]).then_inc(q_split, 1)
                dve.wait_ge(q_split, 3 * b + 2)
                dve.tensor_tensor(q_parts[:, i, 2], q_res[:], q_parts[:, i, 1], ALU.subtract).then_inc(q_split, 1)
                dve.wait_ge(v_ps_ok, b + 1)
                if b >= 2:
                    dve.wait_ge(v_out[b - 2], 16)
                dve.tensor_tensor(v_nat[:, i], s_ps[:, i].rearrange("p (t m) -> p t m", m=D),
                                  bias_bc[:, 0].unsqueeze(1).to_broadcast([128, TILES, D]), ALU.add).then_inc(v_nat_ok, 1)

            def maximum(g, q, m):
                p, qt, u = m // 8, m // 2 % 4, m % 2
                dve.wait_ge(scores_ready, 16 * g + m + 1)
                dve.tensor_reduce(neg_max[:, q, u, 4 * p + qt:4 * p + qt + 1], s_ps[:, m % 2], AX.X, ALU.max, negate=True)\
                   .then_inc(max_done, 1)

            def transpose_max(g, q):
                dve.wait_ge(split_step, 4 * g + 4)
                dve.transpose(m_rows[:, q].rearrange("p a r -> p (a r)"),
                              m_src[:].rearrange("p u k -> p (u k)")).then_inc(rows_ready, 1)

            def normalize(oct_i, o):
                yT = mi_ps[:].rearrange("p (t h n) -> p t h n", t=TILES, n=16)
                dve.wait_ge(yT_ready, oct_i + 1)
                dve.reciprocal(y_rec[:], yT[:, :, :, DK]).then_inc(rec_done, 1)
                dve.wait_ge(rec_done, oct_i + 1)
                dve.tensor_tensor(attn[:, :, o], yT[:, :, :, 0:DK], y_rec[:].unsqueeze(3).to_broadcast([128, TILES, 8, DK]),
                                  ALU.mult).then_inc(norm_done, 1)

            def residual(ln, other):
                dve.tensor_tensor(res[:], mi_ps[:].rearrange("p (t m) -> p t m", m=D), other, ALU.add).then_inc(res_done, 1)
                dve.wait_ge(res_done, ln + 1)
                for t in range(TILES):
                    ins = dve.bn_stats(stats[:, t], res[:, t])
                ins.then_inc(stats_done, 1)
                dve.wait_ge(stats_done, ln + 1)
                dve.nop(nofuse=True)
                for t in range(TILES):
                    ins = dve.bn_aggr(mv[:, t], stats[:, t])
                ins.then_inc(mv_done, 1)

            def layernorm(ln, dst):
                dve.wait_ge(rstd_done, ln + 1)
                for t in range(TILES):
                    ins = dve.tensor_scalar(dst[:, t], res[:, t], mv[:, t, 0:1], rstd[:, t:t + 1], ALU.subtract, ALU.mult)
                ins.then_inc(ln_done, 1)

            def attn_residual(b, bi):
                dve.wait_ge(proj_ready, b + 1)
                residual(2 * b, x_bo[:, bi])

            def ffn_residual(b):
                dve.wait_ge(x1b_done, b + 1)
                dve.wait_ge(y2_ready, b + 1)
                residual(2 * b + 1, x1_b2[:])

            def batch(b, first, last):
                for q in range(G):
                    g = G * b + q
                    for m in range(16):
                        if m == 3 and not (last and q == G - 1):
                            transpose_max(g + 1, (q + 1) % G)
                        if m == 12 and q == 0 and not first:
                            normalize(2 * b - 1, 1)
                        if m == 12 and q == 1 and not first:
                            attn_residual(b - 1, b - 1)
                        if m == 12 and q == 2:
                            normalize(2 * b, 0)
                        if not (last and q >= 2):
                            maximum(g + 2, (q + 2) % G, m)
                    if q == 1 and not first:
                        layernorm(2 * b - 2, x1[:])
                if not first:
                    ffn_residual(b - 1)
                    layernorm(2 * b - 1, x2[:, b - 1])

            dve.wait_ge(qk_in[0], 64)
            dve.wait_ge(fill_in, 16 * 4 * B)

            def first_slots(q):
                for slot, src in ((q_slot, q_all), (k_slot, k_all)):
                    for p in range(2):
                        ins = dve.tensor_copy(*slot_and_source(slot, src, q, p, 0))
                ins.then_inc(slots_first, 1)

            for q in range(G):
                first_slots(q)
            for m in range(16):
                maximum(0, 0, m)
            transpose_max(0, 0)
            for m in range(16):
                maximum(1, 1, m)
            dve.wait_ge(x_bo_ok, B)
            batch(0, True, False)
            with dve.Fori(1, B - 1) as b:
                batch(b, False, False)
            batch(B - 1, False, True)
            normalize(2 * B - 1, 1)
            attn_residual(B - 1, B - 1)
            layernorm(2 * B - 2, x1[:])
            ffn_residual(B - 1)
            layernorm(2 * B - 1, x2[:, B - 1])

        @block.tensor
        def _(pe):
            pe.wait_ge(ident_ok, 2)
            pe.wait_ge(consts_ok, 1)
            pe.wait_ge(ld_w, 64)
            for i in range(3):
                pe.transpose(st_ps[:, 0, 0, 128 * i:128 * i + 128], w_nat[:, i], ident[:])
            pe.wait_ge(wo_ok, 4)
            pe.transpose(st_ps[:, 0, 0, 384:512], wo_perm[:], ident[:]).then_inc(wT_ps_ok, 1)
            pe.wait_ge(rot_ok, 3)
            pe.matmul(mi_ps[:, 0:1], g_row[:].rearrange("o c j i -> o (c j i)"), one[:], start=True, stop=True).then_inc(g_ps_ok, 1)
            pe.wait_ge(g_ok, 1)
            for b in range(B):
                i = b % 2
                xb = o_ps if i else mi_ps
                pe.wait_ge(ld_x[b], 16)
                for t in range(TILES):
                    ins = pe.transpose(xb[:, 128 * t:128 * t + 128], x_nat[:, b, t], ident[:])
                ins.then_inc(xT_ps_ok, 1)
                pe.wait_ge(xT_ok, b + 1)
                if b == 0:
                    pe.wait_ge(wT_ok, 1)
                if b >= 2:
                    pe.wait_ge(qf_ok, 2 * b - 2)
                    pe.wait_ge(kf_ok, 2 * b - 2)
                    pe.wait_ge(v_nat_ok, b - 1)
                pe.matmul(st_ps[:, 0, i], wT[:, 0], xT[:, b], start=True, stop=True).then_inc(qk_ps_ok, 1)
                pe.matmul(st_ps[:, 1, i], wT[:, 1], xT[:, b], start=True, stop=True).then_inc(qk_ps_ok, 1)
                for t in range(TILES):
                    ins = pe.matmul(s_ps[:, i, 128 * t:128 * t + 128], xT[:, b, 128 * t:128 * t + 128], wT[:, 2],
                                    start=True, stop=True)
                ins.then_inc(v_ps_ok, 1)
            pe.wait_ge(qf_ok, 2 * B)
            pe.wait_ge(kf_ok, 2 * B)
            pe.wait_ge(v_nat_ok, B)

            def score(g, q, m, free):
                p, qt, u = m // 8, m // 2 % 4, m % 2
                if free:
                    pe.wait_ge(max_done, 16 * g + m - 1)
                rows = half(u, KS)
                pe.matmul(s_ps[:, m % 2], q_slot[rows, q, p, 128 * qt:128 * qt + 128], k_slot[rows, q, p],
                          start=True, stop=True).then_inc(scores_ready, 1)

            def score_t(g, q, s, free):
                kt, p = divmod(s, 2)
                if free:
                    pe.wait_ge(exp_done, 8 * g + s - 1)
                for u in range(2):
                    rows = half(u, KM)
                    ins = pe.matmul(st_ps[:, p, u], k_slot[rows, q, p, 128 * kt:128 * kt + 128], q_slot[rows, q, p],
                                    start=True, stop=True)
                ins.then_inc(st_ready, 1)

            def values(g, q, kt):
                pe.wait_ge(exp_done, 8 * g + 2 * kt + 2)
                for j in range(4):
                    ins = pe.matmul(o_ps[32 * j:32 * j + 32], v_slot[:, q, j, kt], probs[:, kt % 2, j // 2, j % 2],
                                    start=(q % 2 == 0 and kt == 0), stop=(q % 2 == 1 and kt == 3))
                ins.then_inc(pv_done, 1)

            def transpose_y(oct_i):
                pe.wait_ge(o_copied, oct_i + 1)
                for t in range(TILES):
                    ins = pe.transpose(mi_ps[:, 128 * t:128 * t + 128], y_raw[:, 128 * t:128 * t + 128], ident[:])
                ins.then_inc(yT_ready, 1)

            def transpose_attn(b):
                pe.wait_ge(norm_done, 2 * b + 2)
                for t in range(TILES):
                    ins = pe.transpose(mi_ps[:, 128 * t:128 * t + 128], attn[:, t].rearrange("p o h d -> p (o h d)"), ident[:])
                ins.then_inc(aT_ps_ok, 1)

            def project(b):
                pe.wait_ge(aT_ok, b + 1)
                for t in range(TILES):
                    ins = pe.matmul(mi_ps[:, 128 * t:128 * t + 128], attnT[:, 128 * t:128 * t + 128], wT[:, 3],
                                    start=True, stop=True)
                ins.then_inc(proj_ready, 1)

            def transpose_x1(b):
                pe.wait_ge(ln_done, 2 * b + 1)
                for t in range(TILES):
                    ins = pe.transpose(mi_ps[:, 128 * t:128 * t + 128], x1[:, t], ident[:])
                ins.then_inc(x1T_ps_ok, 1)

            def hidden(b, m):
                pe.wait_ge(x1T_ok, b + 1)
                if m:
                    pe.wait_ge(relu_done, 2 * b + 1)
                pe.matmul(mi_ps[:], w1_sb[:, 128 * m:128 * m + 128], x1T[:], start=True, stop=True).then_inc(hid_ready, 1)

            def ffn_out(b):
                pe.wait_ge(relu_done, 2 * b + 2)
                for t in range(TILES):
                    for m in range(2):
                        ins = pe.matmul(mi_ps[:, 128 * t:128 * t + 128], hidT[:, m, 128 * t:128 * t + 128], w2_sb[:, m],
                                        start=(m == 0), stop=(m == 1))
                ins.then_inc(y2_ready, 1)

            def batch(b, first, last):
                for q in range(G):
                    g = G * b + q
                    if not (last and q >= 2):
                        if first and q < 2:
                            pe.wait_ge(slots_first, g + 3)
                        else:
                            pe.wait_ge(slot_step, g - 1)
                    pe.wait_ge(rows_in[q], 32 * (b + 1))
                    for kt in range(4):
                        for p in range(2):
                            s = 2 * kt + p
                            score_t(g, q, s, not (first and q == 0 and s < 2))
                            if not (last and q >= 2):
                                for m in range(2):
                                    score(g + 2, (q + 2) % G, 2 * s + m, True)
                        if kt == 0 and not (first and q == 0):
                            values(g - 1, (q - 1) % G, 3)
                        if kt == 1 and q % 2 == 0 and not (first and q == 0):
                            pe.wait_ge(o_copied, 2 * b + q // 2)
                        if kt:
                            values(g, q, kt - 1)
                        if (q, kt) == (0, 2) and not first:
                            transpose_y(2 * b - 1)
                        if (q, kt) == (1, 0) and not first:
                            transpose_attn(b - 1)
                        if (q, kt) == (1, 2) and not first:
                            project(b - 1)
                        if (q, kt) == (2, 0) and not first:
                            transpose_x1(b - 1)
                        if (q, kt) == (2, 2):
                            if not first:
                                pe.wait_ge(x1T_ok, b)
                            transpose_y(2 * b)
                        if (q, kt) == (2, 3) and not first:
                            pe.wait_ge(norm_done, 2 * b + 1)
                            hidden(b - 1, 0)
                        if (q, kt) == (3, 1) and not first:
                            hidden(b - 1, 1)
                        if (q, kt) == (3, 3) and not first:
                            ffn_out(b - 1)

            for g in range(2):
                pe.wait_ge(slots_first, g + 1)
                for m in range(16):
                    score(g, g, m, not (g == 0 and m < 2))
            pe.wait_ge(v_zero, 2 + G)
            pe.wait_ge(ld_ffn, 64)
            batch(0, True, False)
            with pe.Fori(1, B - 1) as b:
                batch(b, False, False)
            batch(B - 1, False, True)
            pe.wait_ge(res_done, 2 * B - 2)
            values(N - 1, G - 1, 3)
            transpose_y(2 * B - 1)
            transpose_attn(B - 1)
            project(B - 1)
            transpose_x1(B - 1)
            hidden(B - 1, 0)
            hidden(B - 1, 1)
            ffn_out(B - 1)


_INS = ["L0_attn_x", "L0_attn_wq", "L0_attn_bq", "L0_attn_wk", "L0_attn_bk", "L0_attn_wv", "L0_attn_bv", "L0_attn_wo",
        "L0_attn_bo", "L0_attn_rot_cos", "L0_attn_rot_sin", "L0_ffn_W1", "L0_ffn_b1", "L0_ffn_W2", "L0_ffn_b2"]


def kernel(**inputs):
    import numpy as _np
    import concourse.bacc as _bacc
    from concourse import mybir as _mybir
    from concourse.bass_utils import run_bass_kernel_spmd as _run

    nc = _bacc.Bacc("TRN2", target_bir_lowering=False, num_devices=1)
    arrays, args = {}, []
    for name in _INS:
        a = _np.ascontiguousarray(inputs[name])
        arrays[f"in_{name}"] = a
        args.append(nc.dram_tensor(f"in_{name}", a.shape, _mybir.dt.from_np(a.dtype), kind="ExternalInput").ap())
    args.append(nc.dram_tensor("out_0", (B, T, D), _mybir.dt.float32, kind="ExternalOutput").ap())
    build_layer(nc, *args)
    r = _run(nc, [arrays], core_ids=[0])
    return r.results[0]["out_0"]
```

```python
from contextlib import ExitStack

import numpy as np

import concourse.bass as bass
from concourse import mybir

F32 = mybir.dt.float32
BF16 = mybir.dt.bfloat16
ALU = mybir.AluOpType
ACT = mybir.ActivationFunctionType
AX = mybir.AxisListType

B, T, D = 4, 512, 128
H, DK = 16, 8
E_SEL, HID = 1, 256
R, C = T // H, D // DK
TILES = T // 128
G = 4
J = H // G
N = B * G
TERMS = 6
KP = TERMS * DK
KM = 96
KS = KM - 3
K0 = 64
MROWS = 24
EPS = 1e-5


def build_layer(nc, x, wq, bq, wk, bk, wv, bv, wo, bo, rot_cos, rot_sin, w1, b1, w2, b2, out):
    with ExitStack() as ctx:
        def sb(name, shape, dt=F32):
            return ctx.enter_context(nc.sbuf_tensor(name, shape, dt))

        def ps(name, shape, dt=F32):
            return ctx.enter_context(nc.psum_tensor(name, shape, dt))

        def sem(name):
            return ctx.enter_context(nc.semaphore(name))

        q_dram = nc.dram_tensor("q_dram", (B, 128, TERMS, T), BF16, kind="Internal").ap()
        k_dram = nc.dram_tensor("k_dram", (B, 128, TERMS, T), BF16, kind="Internal").ap()
        v_dram = nc.dram_tensor("v_dram", (B, T, D), F32, kind="Internal").ap()
        m_dram = nc.dram_tensor("m_dram", (G, 2, MROWS, 4, R), BF16, kind="Internal").ap()

        x_nat = sb("x_nat", [128, B, TILES, D])
        hidT = sb("hidT", [128, 2, T])
        w_nat = hidT[:, 0].rearrange("p (a m) -> p a m", a=4)
        wo_perm = sb("wo_perm", [128, 128])
        wT = sb("wT", [128, 4, 128])
        w1_sb = sb("w1_sb", [128, HID])
        w2_sb = sb("w2_sb", [128, 2, D])
        b1_sb = sb("b1_sb", [128, 2])
        bias_bc = sb("bias_bc", [128, 3, D])
        bqk = sb("bqk", [128, 2])
        rot = sb("rot", [1, 2, DK // 2])
        rot_sq = sb("rot_sq", [1, 2, DK // 2])
        rot_g = sb("rot_g", [1, DK // 2])
        g_row = sb("g_row", [1, C, DK // 2, 2])
        g_col = sb("g_col", [128, 1])
        bq_g = sb("bq_g", [128, 1])
        one = sb("one", [1, 1])
        ident = sb("ident", [128, 128])
        bv_perm = sb("bv_perm", [128, D])
        q_parts = sb("q_parts", [128, B, 3, T], BF16)
        k_parts = sb("k_parts", [128, B, 3, T], BF16)
        v_nat = sb("v_nat", [128, B, TILES, D])
        qk_all = sb("qk_all", [128, B, C, T], BF16)
        q_slot = sb("q_slot", [KM, G, J, T], BF16)
        k_slot = sb("k_slot", [KM, G, J, T], BF16)
        v_all = sb("v_all", [128, B, H, 4 * DK])
        v_slot = sb("v_slot", [128, G, J, 4, 32])
        neg_max = sb("neg_max", [128, G, 2, 8])
        m_res = sb("m_res", [128, 2, 8])
        m_src = sb("m_src", [128, 2, 32], BF16)
        m_rows = sb("m_rows", [128, G, 2, 32], BF16)
        probs = sb("probs", [128, 4, J, T])
        xT, qf, kf = probs[:, 0], probs[:, 1], probs[:, 2]
        q_res, k_res = probs[:, 3, 0], probs[:, 3, 1]
        y_raw = sb("y_raw", [128, T])
        y_rec = sb("y_rec", [128, TILES, 8])
        attn = sb("attn", [128, TILES, 2, 8, DK])
        attnT, x1T = v_nat[:, 0].rearrange("p t m -> p (t m)"), v_nat[:, 1].rearrange("p t m -> p (t m)")
        x1, x1_b2 = v_nat[:, 2], v_nat[:, 3]
        res = sb("res", [128, TILES, D])
        stats = sb("stats", [128, TILES, 6])
        mv = sb("mv", [128, TILES, 2])
        var_eps = sb("var_eps", [128, TILES])
        minus_half = sb("minus_half", [128, TILES])
        rstd = sb("rstd", [128, TILES])
        x2 = sb("x2", [128, TILES, D])

        st_ps = ps("st_ps", [128, 2, 2, T])
        s_ps = ps("s_ps", [128, 2, T])
        o_ps = ps("o_ps", [128, T])
        mi_ps = ps("mi_ps", [128, T])

        ld_w = sem("ld_w")
        ld_wo = sem("ld_wo")
        ld_small = sem("ld_small")
        ld_bias = sem("ld_bias")
        ld_x = [sem(f"ld_x{b}") for b in range(B)]
        ld_ffn = sem("ld_ffn")
        ident_ok = sem("ident_ok")
        consts_ok = sem("consts_ok")
        rot_ok = sem("rot_ok")
        g_ps_ok = sem("g_ps_ok")
        g_ok = sem("g_ok")
        wT_ps_ok = sem("wT_ps_ok")
        wT_ok = sem("wT_ok")
        wo_ok = sem("wo_ok")
        xT_ps_ok = sem("xT_ps_ok")
        xT_ok = sem("xT_ok")
        qk_ps_ok = sem("qk_ps_ok")
        v_ps_ok = sem("v_ps_ok")
        qf_ok = sem("qf_ok")
        kf_ok = sem("kf_ok")
        v_nat_ok = sem("v_nat_ok")
        q_split = sem("q_split")
        k_split = sem("k_split")
        q_out = [sem(f"q_out{b}") for b in range(B)]
        k_out = [sem(f"k_out{b}") for b in range(B)]
        v_out = [sem(f"v_out{b}") for b in range(B)]
        qk_first = sem("qk_first")
        qk_in = [sem(f"qk_in{b}") for b in range(B)]
        v_in = [sem(f"v_in{b}") for b in range(B)]
        q_fill = sem("q_fill")
        k_fill = sem("k_fill")
        bv_ok = sem("bv_ok")
        x_bo_ok = sem("x_bo_ok")
        v_zero = sem("v_zero")
        scores_ready = sem("scores_ready")
        max_done = sem("max_done")
        split_step = sem("split_step")
        rows_ready = sem("rows_ready")
        rows_out = [sem(f"rows_out{q}") for q in range(G)]
        rows_in = [sem(f"rows_in{q}") for q in range(G)]
        st_ready = sem("st_ready")
        exp_done = sem("exp_done")
        pv_done = sem("pv_done")
        o_copied = sem("o_copied")
        yT_ready = sem("yT_ready")
        rec_done = sem("rec_done")
        norm_done = sem("norm_done")
        aT_ps_ok = sem("aT_ps_ok")
        aT_ok = sem("aT_ok")
        slot_0 = sem("slot_0")
        slots_first = sem("slots_first")
        q_refilled = sem("q_refilled")
        k_refilled = sem("k_refilled")
        proj_ready = sem("proj_ready")
        res_done = sem("res_done")
        stats_done = sem("stats_done")
        mv_done = sem("mv_done")
        var_done = sem("var_done")
        rstd_done = sem("rstd_done")
        centred = sem("centred")
        ln_done = sem("ln_done")
        x1b_done = sem("x1b_done")
        x1T_ps_ok = sem("x1T_ps_ok")
        x1T_ok = sem("x1T_ok")
        hid_ready = sem("hid_ready")
        relu_done = sem("relu_done")
        y2_ready = sem("y2_ready")
        x2_free = sem("x2_free")

        block = ctx.enter_context(nc.Block())

        Q_RUNS = {1: ((2, 3),), 2: ((1, 1), (5, 1)), 3: ((0, 1),)}
        K_RUNS = {1: ((0, 3),), 2: ((4, 2),), 3: ((3, 1),)}
        Q_OUT, K_OUT = (16 * sum(len(runs) for runs in of.values()) for of in (Q_RUNS, K_RUNS))
        N_SMALL, N_BIAS = 4, 3

        def slot_and_source(slot, p0, q, bi, j0=0, j1=J):
            return (slot[0:KP, q, j0:j1].rearrange("p j (c r) -> p j c r", c=C),
                    qk_all[p0:p0 + KP, bi, :, 128 * q + R * j0:128 * q + R * j1].rearrange("p c (j r) -> p j c r", r=R))

        @block.sync
        def _(sp):
            def load_x(b):
                sp.dma_start(x_nat[:, b], x[b].rearrange("(t p) m -> p t m", p=128)).then_inc(ld_x[b], 16)

            load_x(0)
            for i, t in enumerate((rot_cos, rot_sin)):
                row = min(T, t.shape[0] - 1)
                sp.dma_start(rot[:, i], t[row:row + 1]).then_inc(ld_small, 16)
            for i, t in enumerate((bq, bk)):
                sp.dma_start(bqk[:, i:i + 1], t.rearrange("(p o) -> p o", o=1)).then_inc(ld_small, 16)
            sp.dma_start(w_nat[:, 3], wo).then_inc(ld_wo, 16)
            load_x(1)
            for i, w in enumerate((bv, bo, b2[E_SEL])):
                sp.dma_start(bias_bc[:, i], w.partition_broadcast(128)).then_inc(ld_bias, 16)
            load_x(2)
            load_x(3)
            sp.dma_start(w1_sb[:], w1[E_SEL]).then_inc(ld_ffn, 16)
            sp.dma_start(w2_sb[:], w2[E_SEL].rearrange("(m p) n -> p m n", p=128)).then_inc(ld_ffn, 16)
            for m in range(2):
                sp.dma_start(b1_sb[:, m:m + 1], b1[E_SEL, 128 * m:128 * m + 128].rearrange("(p o) -> p o", o=1)).then_inc(ld_ffn, 16)

            def parts_out(tensor, parts, dram, b, part, out):
                for t0, n in (Q_RUNS if tensor == "q" else K_RUNS)[part]:
                    sp.dma_start(dram[b, :, t0:t0 + n],
                                 parts[:, b, part - 1].unsqueeze(1).to_broadcast([128, n, T])).then_inc(out[b], 16)

            def write_out(b):
                sp.wait_ge(qf_ok, 2 * b + 2)
                parts_out("q", q_parts, q_dram, b, 1, q_out)
                sp.wait_ge(kf_ok, 2 * b + 2)
                parts_out("k", k_parts, k_dram, b, 1, k_out)
                sp.wait_ge(q_split, 3 * b + 2)
                parts_out("q", q_parts, q_dram, b, 2, q_out)
                sp.wait_ge(q_split, 3 * b + 3)
                parts_out("q", q_parts, q_dram, b, 3, q_out)
                sp.wait_ge(k_split, 3 * b + 2)
                parts_out("k", k_parts, k_dram, b, 2, k_out)
                sp.wait_ge(k_split, 3 * b + 3)
                parts_out("k", k_parts, k_dram, b, 3, k_out)

            def write_v(b):
                sp.wait_ge(v_nat_ok, b + 1)
                sp.dma_start(v_dram[b].rearrange("(t p) m -> p t m", p=128), v_nat[:, b]).then_inc(v_out[b], 16)

            def read_back(b, n0=0):
                sp.wait_ge(q_out[b], Q_OUT)
                sp.dma_start(qk_all[0:KP, b, :, n0:T],
                             q_dram[b].rearrange("(c d) t n -> (d t) c n", d=DK)[:, :, n0:T]).then_inc(qk_in[b], 16)
                sp.wait_ge(k_out[b], K_OUT)
                sp.dma_start(qk_all[K0:K0 + KP, b, :, n0:T],
                             k_dram[b].rearrange("(c d) t n -> (d t) c n", d=DK)[:, :, n0:T]).then_inc(qk_in[b], 16)

            def read_first():
                for out, slots, dram, p0 in ((q_out, Q_OUT, q_dram, 0), (k_out, K_OUT, k_dram, K0)):
                    sp.wait_ge(out[0], slots)
                    sp.dma_start(qk_all[p0:p0 + KP, 0, :, 0:128],
                                 dram[0].rearrange("(c d) t n -> (d t) c n", d=DK)[:, :, 0:128]).then_inc(qk_first, 16)

            def read_v(b):
                sp.wait_ge(v_out[b], 16)
                for cl in range(4):
                    src = v_dram[b].rearrange("(h r) m -> r h m", r=R)[:, :, 32 * cl:32 * cl + 32]
                    sp.dma_start(v_all[32 * cl:32 * cl + 32, b], src).then_inc(v_in[b], 16)

            def rows_to_slot(q, count, b):
                sp.wait_ge(rows_ready, count)
                for cl in range(4):
                    sp.dma_start(m_dram[q, :, :, cl].rearrange("u k r -> k u r"),
                                 m_rows[32 * cl:32 * cl + MROWS, q]).then_inc(rows_out[q], 16)
                sp.wait_ge(rows_out[q], 64 * (b + 1))
                sp.dma_start(q_slot[KS:KM, q].rearrange("k (a j) n -> k a (j n)", a=2),
                             m_dram[q].rearrange("a (k n) c r -> k a (n c r)", k=3)).then_inc(rows_in[q], 16)

            def store(b, bi):
                sp.wait_ge(ln_done, 2 * b + 2)
                sp.dma_start(out[bi].rearrange("(t p) m -> p t m", p=128), x2[:]).then_inc(x2_free, 16)

            def batch(b, first, last):
                for q in range(G):
                    if not (last and q == G - 1):
                        rows_to_slot((q + 1) % G, b * G + q + 2, b + (q + 1) // G)
                    if first and q < 2:
                        read_back(q + 2)
                        read_v(q + 2)
                if not first:
                    store(b - 1, b - 1)

            write_out(0)
            read_first()
            read_back(0, 128)
            write_v(0)
            write_out(1)
            write_v(1)
            read_v(0)
            write_out(2)
            write_v(2)
            rows_to_slot(0, 1, 0)
            read_back(1)
            read_v(1)
            write_out(3)
            write_v(3)
            batch(0, True, False)
            with sp.Fori(1, B - 1) as b:
                batch(b, False, False)
            batch(B - 1, False, True)
            for t in range(TILES):
                sp.wait_ge(ln_done, 2 * B - 2 + TILES + t + 1)
                sp.dma_start(out[B - 1, 128 * t:128 * t + 128], x2[:, t]).then_inc(x2_free, 16)
            sp.wait_ge(x2_free, 16 * (B + TILES))

        @block.gpsimd
        def _(pool):
            pool.memset(one[:], 1.0).then_inc(consts_ok, 1)
            pool.memset(ident[:], 0.0).then_inc(ident_ok, 1)
            pool.wait_ge(ident_ok, 1)
            pool.affine_select(out=ident[:], in_=ident[:], compare_op=ALU.not_equal, fill=1.0, base=0,
                               pattern=[[-1, 128]], channel_multiplier=1).then_inc(ident_ok, 1)
            for q in range(G):
                pool.memset(q_slot[:, q], 0.0).then_inc(q_fill, 1)
            pool.wait_ge(ld_wo, 16)
            for o in range(2):
                pool.tensor_copy(wo_perm[:].rearrange("p (o j u d) -> p o j u d", o=2, j=J, u=2)[:, o],
                                 w_nat[:, 3].rearrange("p (o u j d) -> p o j u d", o=2, j=J, u=2)[:, o]).then_inc(wo_ok, 1)
            pool.memset(m_src[:], 0.0).then_inc(consts_ok, 1)
            pool.memset(minus_half[:], -0.5).then_inc(consts_ok, 1)
            pool.memset(x2[:], 0.0).then_inc(x2_free, 16)
            pool.memset(v_slot[:], 0.0).then_inc(v_zero, 1)
            pool.wait_ge(v_zero, 1)
            for q in range(G):
                c0 = 16 * (q % 2) + DK
                pool.memset(v_slot[:, q, :, :, c0:c0 + 1], 1.0).then_inc(v_zero, 1)
            pool.memset(k_slot[:, 3], 1.0).then_inc(k_fill, 1)

            def split(b, full, parts, rest, done):
                pool.wait_ge(done, 3 * b)
                pool.tensor_tensor(rest, full[:, b], parts[:, b, 0], ALU.subtract).then_inc(done, 1)
                pool.wait_ge(done, 3 * b + 1)
                pool.tensor_copy(parts[:, b, 1], rest).then_inc(done, 1)
                pool.wait_ge(done, 3 * b + 2)
                pool.tensor_tensor(parts[:, b, 2], rest, parts[:, b, 1], ALU.subtract).then_inc(done, 1)

            for b in range(1, B):
                pool.wait_ge(kf_ok, 2 * b + 2)
                split(b, kf, k_parts, k_res, k_split)

            def copy_v(q, bi):
                c0 = 16 * (q % 2)
                return pool.tensor_copy(v_slot[:, q, :, :, c0:c0 + DK].rearrange("p j k n -> p (j k) n"),
                                        v_all[:, bi, J * q:J * q + J].rearrange("p j (k d) -> p (j k) d", d=DK))

            def split_max(g, q):
                nm, r1 = neg_max[:, q], m_res[:]
                part = [m_src[:, :, 8 * i:8 * i + 8] for i in range(3)]
                pool.wait_ge(max_done, 16 * g + 16)
                pool.nop(nofuse=True)
                pool.tensor_copy(part[0], nm).then_inc(split_step, 1)
                pool.wait_ge(split_step, 4 * g + 1)
                pool.tensor_tensor(r1, nm, part[0], ALU.subtract).then_inc(split_step, 1)
                pool.wait_ge(split_step, 4 * g + 2)
                pool.nop(nofuse=True)
                pool.tensor_copy(part[1], r1).then_inc(split_step, 1)
                pool.wait_ge(split_step, 4 * g + 3)
                pool.tensor_tensor(part[2], r1, part[1], ALU.subtract).then_inc(split_step, 1)

            def refill(g, q, bi):
                pool.wait_ge(st_ready, 8 * g + 8)
                pool.nop(nofuse=True)
                for j in range(J):
                    pool.tensor_copy(*slot_and_source(q_slot, 0, q, bi, j, j + 1))
                pool.wait_ge(pv_done, 4 * g + 4)
                pool.nop(nofuse=True)
                copy_v(q, bi).then_inc(q_refilled, 1)

            def inv_std(ln):
                pool.wait_ge(mv_done, ln + 1)
                pool.nop(nofuse=True)
                pool.tensor_scalar(var_eps[:], mv[:, :, 1], EPS, None, ALU.add).then_inc(var_done, 1)
                pool.wait_ge(var_done, ln + 1)
                pool.tensor_tensor(rstd[:], var_eps[:], minus_half[:], ALU.pow).then_inc(rstd_done, 1)

            def layernorm(ln, dst):
                inv_std(ln)
                pool.wait_ge(rstd_done, ln + 1)
                pool.tensor_tensor(res[:], res[:], mv[:, :, 0].unsqueeze(2).to_broadcast([128, TILES, D]),
                                   ALU.subtract).then_inc(centred, 1)
                pool.wait_ge(centred, ln + 1)
                pool.tensor_tensor(dst, res[:], rstd[:].unsqueeze(2).to_broadcast([128, TILES, D]), ALU.mult).then_inc(ln_done, 1)

            def add_b2(ln, count=1):
                pool.wait_ge(ln_done, ln + count)
                pool.tensor_tensor(x1_b2, x1, bias_bc[:, 2].unsqueeze(1).to_broadcast([128, TILES, D]),
                                   ALU.add).then_inc(x1b_done, 1)

            def batch(b, first, last):
                for q in range(G):
                    g = G * b + q
                    if first and q == 1:
                        pool.wait_ge(qk_in[1], 32)
                        pool.wait_ge(v_in[1], 64)
                    if not (first and q == 0) and not (last and q):
                        refill(g - 1, (q - 1) % G, b + 1 if q else b)
                    if q == 1 and not first:
                        layernorm(2 * b - 2, x1)
                    if q == 3 and not first:
                        pool.wait_ge(x2_free, 16 * b)
                        layernorm(2 * b - 1, x2[:])
                    if not (last and q >= 2):
                        split_max(g + 2, (q + 2) % G)
                    if q == 2 and not first:
                        add_b2(2 * b - 2)

            pool.wait_ge(v_in[0], 64)
            pool.wait_ge(v_zero, 1 + G)
            for q in range(G):
                ins = copy_v(q, 0)
            ins.then_inc(v_zero, 1)
            split_max(0, 0)
            pool.wait_ge(qf_ok, 2 * B)
            split(B - 1, qf, q_parts, q_res, q_split)
            split_max(1, 1)
            pool.wait_ge(ld_bias, 16 * N_BIAS)
            for b in range(B):
                pool.wait_ge(xT_ps_ok, b + 1)
                pool.tensor_tensor(x_nat[:, b], x_nat[:, b], bias_bc[:, 1].unsqueeze(1).to_broadcast([128, TILES, D]),
                                   ALU.add).then_inc(x_bo_ok, 1)
            batch(0, True, False)
            for b in range(2, B):
                pool.wait_ge(qk_in[b], 32)
                pool.wait_ge(v_in[b], 64)
            with pool.Fori(1, B - 1) as b:
                batch(b, False, False)
            batch(B - 1, False, True)
            inv_std(2 * B - 2)
            add_b2(2 * B - 2, TILES)
            inv_std(2 * B - 1)

        @block.scalar
        def _(act):
            for i, w in enumerate((wq, wk, wv)):
                act.dma_start(w_nat[:, i], w).then_inc(ld_w, 16)
            def copy_x(b):
                act.wait_ge(xT_ps_ok, b + 1)
                act.copy(xT[:, b], (o_ps if b % 2 else mi_ps)[:]).then_inc(xT_ok, 1)

            copy_x(0)
            act.wait_ge(wT_ps_ok, 1)
            for i in range(3):
                src = s_ps[:, 0, 128 * i:128 * i + 128]
                if i == 2:
                    act.copy(wT[:, i].rearrange("p (c t d) -> p c t d", c=4, t=4),
                             src.rearrange("p (t c d) -> p c t d", c=4, t=4)).then_inc(wT_ok, 1)
                else:
                    act.copy(wT[:, i], src).then_inc(wT_ok, 1)

            def project_qk(b):
                i = b % 2
                if b == 0:
                    act.wait_ge(g_ok, 2)
                act.wait_ge(qk_ps_ok, 2 * b + 1)
                act.activation(qf[:, b], st_ps[:, 0, i], ACT.Identity, bias=bq_g[:], scale=g_col[:]).then_inc(qf_ok, 1)
                act.activation(q_parts[:, b, 0], st_ps[:, 0, i], ACT.Identity, bias=bq_g[:], scale=g_col[:]).then_inc(qf_ok, 1)
                if b < B - 1:
                    copy_x(b + 1)
                act.wait_ge(qk_ps_ok, 2 * b + 2)
                act.activation(kf[:, b], st_ps[:, 1, i], ACT.Identity, bias=bqk[:, 1:2]).then_inc(kf_ok, 1)
                act.activation(k_parts[:, b, 0], st_ps[:, 1, i], ACT.Identity, bias=bqk[:, 1:2]).then_inc(kf_ok, 1)

            def first_slots(q):
                act.copy(*slot_and_source(q_slot, 0, q, 0))
                act.copy(*slot_and_source(k_slot, K0, q, 0)).then_inc(slots_first, 1)

            for b in range(B):
                project_qk(b)
            act.wait_ge(wT_ps_ok, 2)
            act.copy(wT[:, 3], o_ps[:, 0:128]).then_inc(wT_ok, 1)
            act.wait_ge(qk_in[0], 32)
            act.wait_ge(q_fill, G)
            act.wait_ge(k_fill, G)
            for q in range(1, G):
                first_slots(q)
            act.wait_ge(q_split, 3 * B)
            act.wait_ge(k_split, 3 * B)

            def group(g, q, b, first, last):
                for s in range(8):
                    kt, p = divmod(s, 2)
                    act.wait_ge(st_ready, 8 * g + s + 1)
                    if not (first and q == 0):
                        act.wait_ge(pv_done, 4 * g + kt - 3)
                    act.activation(probs[:, kt, 2 * p:2 * p + 2], st_ps[:, p], ACT.Exp).then_inc(exp_done, 1)
                    if s in (1, 3, 5, 6) and not (first and q == 0) and not (last and q):
                        if first and q == 1 and s == 1:
                            act.wait_ge(qk_in[1], 32)
                        j = (s + 1) // 2 - (s < 6)
                        ins = act.copy(*slot_and_source(k_slot, K0, (q - 1) % G, b + 1 if q else b, j, j + 1))
                        if j == J - 1:
                            ins.then_inc(k_refilled, 1)
                    if s == (1 if last and q == 2 else 2) and q % 2 == 0 and not (first and q == 0):
                        copy_o(2 * b + q // 2 - 1, 4 * g, first)
                    if not first:
                        if (q, s) == (1, 0):
                            copy_aT(b - 1)
                        if (q, s) == (2, 2):
                            copy_x1T(b - 1)
                        if (q, s) == (2, 6):
                            relu(b - 1, 0)
                        if (q, s) == (3, 0):
                            relu(b - 1, 1)

            def copy_o(oct_i, count, first):
                act.wait_ge(pv_done, count)
                if not first:
                    act.wait_ge(yT_ready, oct_i)
                act.copy(y_raw[:].rearrange("p (r c) -> p c r", c=C), o_ps[:].rearrange("p (c r) -> p c r", c=C))\
                   .then_inc(o_copied, 1)

            def copy_aT(b):
                act.wait_ge(aT_ps_ok, b + 1)
                act.copy(attnT, mi_ps[:]).then_inc(aT_ok, 1)

            def copy_x1T(b):
                act.wait_ge(x1T_ps_ok, b + 1)
                act.copy(x1T, mi_ps[:]).then_inc(x1T_ok, 1)

            def relu(b, m):
                act.wait_ge(hid_ready, 2 * b + m + 1)
                act.activation(hidT[:, m], mi_ps[:], ACT.Relu, bias=b1_sb[:, m:m + 1]).then_inc(relu_done, 1)

            def batch(b, first, last):
                for q in range(G):
                    group(G * b + q, q, b, first, last)

            batch(0, True, False)
            for b in range(2, B):
                act.wait_ge(qk_in[b], 32)
            for b in range(B):
                act.wait_ge(v_out[b], 16)
            with act.Fori(1, B - 1) as b:
                batch(b, False, False)
            batch(B - 1, False, True)
            copy_o(2 * B - 1, 4 * N, False)
            for t in range(TILES):
                act.wait_ge(aT_ps_ok, B + t)
                act.copy(attnT[:, 128 * t:128 * t + 128], st_ps[:, t // 2, t % 2, 0:128]).then_inc(aT_ok, 1)
            for t in range(TILES):
                act.wait_ge(x1T_ps_ok, B + t)
                act.copy(x1T[:, 128 * t:128 * t + 128], st_ps[:, t // 2, t % 2, 0:128]).then_inc(x1T_ok, 1)
            for m in range(2):
                act.wait_ge(hid_ready, 2 * B - 1 + m)
                act.activation(hidT[:, m], s_ps[:, m], ACT.Relu, bias=b1_sb[:, m:m + 1]).then_inc(relu_done, 1)

        @block.vector
        def _(dve):
            def fill_k(q):
                dve.memset(k_slot[:, q], 1.0).then_inc(k_fill, 1)

            fill_k(0)
            fill_k(1)
            dve.wait_ge(ld_small, 16 * N_SMALL)
            dve.tensor_tensor(rot_sq[:], rot[:], rot[:], ALU.mult).then_inc(rot_ok, 1)
            dve.wait_ge(rot_ok, 1)
            dve.tensor_tensor(rot_g[:], rot_sq[:, 0], rot_sq[:, 1], ALU.add).then_inc(rot_ok, 1)
            dve.wait_ge(rot_ok, 2)
            dve.tensor_scalar(g_row[:], rot_g[:].unsqueeze(1).unsqueeze(3).to_broadcast([1, C, DK // 2, 2]),
                              float(np.float32(1.0) / np.float32(np.sqrt(DK))), None, ALU.mult).then_inc(rot_ok, 1)
            dve.wait_ge(g_ps_ok, 1)
            dve.tensor_copy(g_col[:], o_ps[:, 0:1]).then_inc(g_ok, 1)
            dve.wait_ge(g_ok, 1)
            dve.tensor_tensor(bq_g[:], bqk[:, 0:1], g_col[:], ALU.mult).then_inc(g_ok, 1)
            dve.wait_ge(ld_bias, 16 * N_BIAS)
            dve.tensor_copy(bv_perm[:].rearrange("p (c t d) -> p c t d", c=4, t=4),
                            bias_bc[:, 0].rearrange("p (t c d) -> p c t d", c=4, t=4)).then_inc(bv_ok, 1)

            fill_k(2)

            def split(b, full, parts, rest, done):
                if b:
                    dve.wait_ge(done, 3 * b)
                dve.tensor_tensor(rest, full[:, b], parts[:, b, 0], ALU.subtract).then_inc(done, 1)
                dve.wait_ge(done, 3 * b + 1)
                dve.tensor_copy(parts[:, b, 1], rest).then_inc(done, 1)
                dve.wait_ge(done, 3 * b + 2)
                dve.tensor_tensor(parts[:, b, 2], rest, parts[:, b, 1], ALU.subtract).then_inc(done, 1)

            def prepare(b):
                if b < B - 1:
                    dve.wait_ge(qf_ok, 2 * b + 2)
                    split(b, qf, q_parts, q_res, q_split)
                if b == 0:
                    dve.wait_ge(kf_ok, 2)
                    split(0, kf, k_parts, k_res, k_split)
                    dve.wait_ge(bv_ok, 1)
                dve.wait_ge(v_ps_ok, b + 1)
                dve.tensor_tensor(v_nat[:, b], s_ps[:, b % 2].rearrange("p (t m) -> p t m", m=D),
                                  bv_perm[:].unsqueeze(1).to_broadcast([128, TILES, D]), ALU.add).then_inc(v_nat_ok, 1)

            def maximum(g, q, m):
                dve.wait_ge(scores_ready, 16 * g + m + 1)
                dve.tensor_reduce(neg_max[:, q, m // 8, m % 8:m % 8 + 1], s_ps[:, m % 2], AX.X, ALU.max, negate=True)\
                   .then_inc(max_done, 1)

            def transpose_max(g, q):
                dve.wait_ge(split_step, 4 * g + 4)
                dve.transpose(m_rows[:, q].rearrange("p a r -> p (a r)"),
                              m_src[:].rearrange("p u k -> p (u k)")).then_inc(rows_ready, 1)

            def yT():
                return mi_ps[:].rearrange("p (t h n) -> p t h n", t=TILES, n=16)

            def invert_sums(oct_i):
                dve.wait_ge(yT_ready, oct_i + 1)
                dve.reciprocal(y_rec[:], yT()[:, :, :, DK]).then_inc(rec_done, 1)

            def normalize(oct_i, o):
                dve.wait_ge(rec_done, oct_i + 1)
                dve.tensor_tensor(attn[:, :, o], yT()[:, :, :, 0:DK], y_rec[:].unsqueeze(3).to_broadcast([128, TILES, 8, DK]),
                                  ALU.mult).then_inc(norm_done, 1)

            def residual(ln, other):
                dve.tensor_tensor(res[:], mi_ps[:].rearrange("p (t m) -> p t m", m=D), other, ALU.add).then_inc(res_done, 1)

            def attn_residual(b, bi):
                dve.wait_ge(proj_ready, b + 1)
                residual(2 * b, x_nat[:, bi])

            def ffn_residual(b):
                dve.wait_ge(ln_done, 2 * b + 1)
                dve.wait_ge(x1b_done, b + 1)
                dve.wait_ge(y2_ready, b + 1)
                residual(2 * b + 1, x1_b2)

            def statistics(ln, t):
                dve.wait_ge(res_done, ln + 1)
                dve.nop(nofuse=True)
                dve.bn_stats(stats[:, t], res[:, t]).then_inc(stats_done, 1)

            def mean_and_variance(ln):
                dve.wait_ge(stats_done, TILES * ln + TILES)
                dve.nop(nofuse=True)
                for t in range(TILES):
                    ins = dve.bn_aggr(mv[:, t], stats[:, t])
                ins.then_inc(mv_done, 1)

            def tail(b, q, m):
                if q == 0 and m == 12:
                    invert_sums(2 * b - 1)
                elif q == 0 and m == 13:
                    normalize(2 * b - 1, 1)
                elif q == 1 and m == 4:
                    attn_residual(b - 1, b - 1)
                elif q == 1 and m in (5, 7, 9, 11):
                    statistics(2 * b - 2, (m - 5) // 2)
                elif q == 1 and m == 12:
                    mean_and_variance(2 * b - 2)
                elif q == 3 and m == 4:
                    ffn_residual(b - 1)
                elif q == 3 and m in (6, 8, 10, 12):
                    statistics(2 * b - 1, (m - 6) // 2)
                elif q == 3 and m == 13:
                    mean_and_variance(2 * b - 1)

            def batch(b, first, last):
                for q in range(G):
                    g = G * b + q
                    for m in range(16):
                        if m == 3 and not (last and q == G - 1):
                            transpose_max(g + 1, (q + 1) % G)
                        if q == 2 and m == 8:
                            invert_sums(2 * b)
                        if q == 2 and m == 10:
                            normalize(2 * b, 0)
                        if not first:
                            tail(b, q, m)
                        if not (last and q >= 2):
                            maximum(g + 2, (q + 2) % G, m)

            for b in range(B):
                prepare(b)
            dve.wait_ge(qk_first, 32)
            dve.wait_ge(q_fill, G)
            dve.wait_ge(k_fill, G)
            dve.tensor_copy(*slot_and_source(q_slot, 0, 0, 0))
            dve.tensor_copy(*slot_and_source(k_slot, K0, 0, 0)).then_inc(slot_0, 1)

            def first_maxima(g):
                for m in range(0, 16, 2):
                    if (g, m) == (1, 4):
                        transpose_max(0, 0)
                    dve.wait_ge(scores_ready, 16 * g + m + 2)
                    dve.tensor_reduce(neg_max[:, g, m // 8, m % 8:m % 8 + 2], st_ps[:, m // 2 % 2], AX.X, ALU.max,
                                      negate=True).then_inc(max_done, 2)

            first_maxima(0)
            first_maxima(1)
            batch(0, True, False)
            dve.wait_ge(x_bo_ok, B)
            with dve.Fori(1, B - 1) as b:
                batch(b, False, False)
            batch(B - 1, False, True)
            invert_sums(2 * B - 1)
            normalize(2 * B - 1, 1)
            dve.wait_ge(ln_done, 2 * B - 2)
            for ln in (2 * B - 2, 2 * B - 1):
                ready = y2_ready if ln % 2 else proj_ready
                other = x1_b2 if ln % 2 else x_nat[:, B - 1]
                if ln % 2:
                    dve.wait_ge(x1b_done, B)
                done = 2 * B - 2 + (TILES if ln % 2 else 0)
                for t in range(TILES):
                    dve.wait_ge(ready, B + t)
                    dve.tensor_tensor(res[:, t], st_ps[:, t // 2, t % 2, 0:D], other[:, t], ALU.add).then_inc(res_done, 1)
                for t in range(TILES):
                    dve.wait_ge(res_done, done + t + 1)
                    dve.bn_stats(stats[:, t], res[:, t]).then_inc(stats_done, 1)
                mean_and_variance(ln)
                dve.wait_ge(rstd_done, ln + 1)
                dst = x2 if ln % 2 else x1
                if ln % 2:
                    dve.wait_ge(x2_free, 16 * B)
                for t in range(TILES):
                    dve.tensor_scalar(dst[:, t], res[:, t], mv[:, t, 0:1], rstd[:, t:t + 1], ALU.subtract, ALU.mult)\
                       .then_inc(ln_done, 1)

        @block.tensor
        def _(pe):
            def transpose_x(b):
                pe.wait_ge(ld_x[b], 16)
                if b >= 2:
                    pe.wait_ge(xT_ok, b - 1)
                for t in range(TILES):
                    ins = pe.transpose((o_ps if b % 2 else mi_ps)[:, 128 * t:128 * t + 128], x_nat[:, b, t], ident[:])
                ins.then_inc(xT_ps_ok, 1)

            pe.wait_ge(ident_ok, 2)
            transpose_x(0)
            pe.wait_ge(ld_w, 48)
            for i in range(3):
                ins = pe.transpose(s_ps[:, 0, 128 * i:128 * i + 128], w_nat[:, i], ident[:])
            ins.then_inc(wT_ps_ok, 1)
            pe.wait_ge(consts_ok, 1)
            pe.wait_ge(rot_ok, 3)
            pe.matmul(o_ps[:, 0:1], g_row[:].rearrange("o c j i -> o (c j i)"), one[:], start=True, stop=True).then_inc(g_ps_ok, 1)

            def project_x(b):
                i = b % 2
                if b == 0:
                    pe.wait_ge(wT_ok, 3)
                pe.wait_ge(xT_ok, b + 1)
                if b >= 2:
                    pe.wait_ge(qf_ok, 2 * b - 2)
                    pe.wait_ge(kf_ok, 2 * b - 2)
                pe.matmul(st_ps[:, 0, i], wT[:, 0], xT[:, b], start=True, stop=True).then_inc(qk_ps_ok, 1)
                if b == 0:
                    pe.wait_ge(g_ok, 1)
                if b < B - 1:
                    transpose_x(b + 1)
                pe.matmul(st_ps[:, 1, i], wT[:, 1], xT[:, b], start=True, stop=True).then_inc(qk_ps_ok, 1)
                if b >= 2:
                    pe.wait_ge(v_nat_ok, b - 1)
                for t in range(TILES):
                    ins = pe.matmul(s_ps[:, i, 128 * t:128 * t + 128], xT[:, b, 128 * t:128 * t + 128], wT[:, 2],
                                    start=True, stop=True)
                ins.then_inc(v_ps_ok, 1)

            for b in range(B):
                project_x(b)
            pe.wait_ge(xT_ok, B)
            pe.wait_ge(wo_ok, 2)
            pe.transpose(o_ps[:, 0:128], wo_perm[:], ident[:]).then_inc(wT_ps_ok, 1)

            def score(g, q, m, free):
                j, qt = divmod(m, 4)
                if free:
                    pe.wait_ge(max_done, 16 * g + m - 1)
                pe.matmul(s_ps[:, m % 2], q_slot[0:KS, q, j, 128 * qt:128 * qt + 128], k_slot[0:KS, q, j],
                          start=True, stop=True).then_inc(scores_ready, 1)

            def score_t(g, q, s, free):
                kt, p = divmod(s, 2)
                if free:
                    pe.wait_ge(exp_done, 8 * g + s - 1)
                for u in range(2):
                    ins = pe.matmul(st_ps[:, p, u], k_slot[:, q, 2 * p + u, 128 * kt:128 * kt + 128], q_slot[:, q, 2 * p + u],
                                    start=True, stop=True)
                ins.then_inc(st_ready, 1)

            def values(g, q, kt, part):
                opens, closes = q % 2 == 0 and kt == 0, q % 2 == 1 and kt == 3
                n0, n1 = (0, T) if opens or closes else (T // 2 * part, T // 2 * part + T // 2)
                if part == 0:
                    pe.wait_ge(exp_done, 8 * g + 2 * kt + 2)
                elif n1 - n0 == T:
                    return
                for j in range(J):
                    ins = pe.matmul(o_ps[32 * j:32 * j + 32, n0:n1], v_slot[:, q, j, kt], probs[:, kt, j, n0:n1],
                                    start=opens, stop=closes)
                if n1 == T:
                    ins.then_inc(pv_done, 1)

            def values_behind(g, q, s, first_of_all):
                kt, part = (s // 2 - 1, 0) if s % 2 else (s // 2 - 2, 1)
                if kt >= 0:
                    values(g, q, kt, part)
                elif not first_of_all:
                    values(g - 1, (q - 1) % G, kt + 4, part)

            def transpose_y(oct_i):
                pe.wait_ge(o_copied, oct_i + 1)
                for t in range(TILES):
                    ins = pe.transpose(mi_ps[:, 128 * t:128 * t + 128], y_raw[:, 128 * t:128 * t + 128], ident[:])
                ins.then_inc(yT_ready, 1)

            def transpose_attn(b):
                pe.wait_ge(norm_done, 2 * b + 2)
                for t in range(TILES):
                    ins = pe.transpose(mi_ps[:, 128 * t:128 * t + 128], attn[:, t].rearrange("p o h d -> p (o h d)"), ident[:])
                ins.then_inc(aT_ps_ok, 1)

            def project(b):
                pe.wait_ge(aT_ok, b + 1)
                for t in range(TILES):
                    ins = pe.matmul(mi_ps[:, 128 * t:128 * t + 128], attnT[:, 128 * t:128 * t + 128], wT[:, 3],
                                    start=True, stop=True)
                ins.then_inc(proj_ready, 1)

            def transpose_x1(b):
                pe.wait_ge(ln_done, 2 * b + 1)
                for t in range(TILES):
                    ins = pe.transpose(mi_ps[:, 128 * t:128 * t + 128], x1[:, t], ident[:])
                ins.then_inc(x1T_ps_ok, 1)

            def hidden(b, m):
                pe.wait_ge(x1T_ok, b + 1)
                if m:
                    pe.wait_ge(relu_done, 2 * b + 1)
                pe.matmul(mi_ps[:], w1_sb[:, 128 * m:128 * m + 128], x1T, start=True, stop=True).then_inc(hid_ready, 1)

            def ffn_out(b):
                pe.wait_ge(relu_done, 2 * b + 2)
                for t in range(TILES):
                    for m in range(2):
                        ins = pe.matmul(mi_ps[:, 128 * t:128 * t + 128], hidT[:, m, 128 * t:128 * t + 128], w2_sb[:, m],
                                        start=(m == 0), stop=(m == 1))
                ins.then_inc(y2_ready, 1)

            def batch(b, first, last):
                for q in range(G):
                    g = G * b + q
                    if not (last and q >= 2):
                        if first and q < 2:
                            pe.wait_ge(slots_first, g + 2)
                        else:
                            pe.wait_ge(q_refilled, g - 1)
                            pe.wait_ge(k_refilled, g - 1)
                    pe.wait_ge(rows_in[q], 16 * (b + 1))
                    for kt in range(4):
                        for p in range(2):
                            s = 2 * kt + p
                            if not (last and q >= 2):
                                score(g + 2, (q + 2) % G, 2 * s, True)
                            score_t(g, q, s, not (first and q == 0 and s < 2))
                            if not (last and q >= 2):
                                score(g + 2, (q + 2) % G, 2 * s + 1, True)
                            if s == 3 and q % 2 == 0 and not (first and q == 0):
                                pe.wait_ge(o_copied, 2 * b + q // 2)
                            values_behind(g, q, s, first and q == 0)
                        if not first:
                            tail(b, q, kt)
                        if (q, kt) == (2, 1):
                            if not first:
                                pe.wait_ge(x1T_ok, b)
                            transpose_y(2 * b)

            def tail(b, q, kt):
                if (q, kt) == (0, 2):
                    transpose_y(2 * b - 1)
                elif (q, kt) == (0, 3):
                    transpose_attn(b - 1)
                elif (q, kt) == (1, 0):
                    project(b - 1)
                elif (q, kt) == (2, 0):
                    transpose_x1(b - 1)
                elif (q, kt) == (2, 2):
                    pe.wait_ge(norm_done, 2 * b + 1)
                    hidden(b - 1, 0)
                elif (q, kt) == (2, 3):
                    hidden(b - 1, 1)
                elif (q, kt) == (3, 0):
                    ffn_out(b - 1)

            pe.wait_ge(qf_ok, 2 * B)
            pe.wait_ge(kf_ok, 2 * B)
            pe.wait_ge(slot_0, 1)
            for g in range(2):
                if g:
                    pe.wait_ge(slots_first, g)
                for m in range(16):
                    j, qt = divmod(m, 4)
                    if m % 2 == 0 and 16 * g + m >= 4:
                        pe.wait_ge(max_done, 16 * g + m - 2)
                    pe.matmul(st_ps[:, m // 2 % 2, m % 2], q_slot[0:KS, g, j, 128 * qt:128 * qt + 128], k_slot[0:KS, g, j],
                              start=True, stop=True).then_inc(scores_ready, 1)
            pe.wait_ge(max_done, 32)
            pe.wait_ge(v_nat_ok, B)
            pe.wait_ge(wT_ok, 4)
            pe.wait_ge(v_zero, 2 + G)
            pe.wait_ge(ld_ffn, 64)
            batch(0, True, False)
            with pe.Fori(1, B - 1) as b:
                batch(b, False, False)
            batch(B - 1, False, True)
            pe.wait_ge(res_done, 2 * B - 2)
            values(N - 1, G - 1, 2, 1)
            values(N - 1, G - 1, 3, 0)
            transpose_y(2 * B - 1)
            tile = [st_ps[:, t // 2, t % 2, 0:128] for t in range(TILES)]
            pe.wait_ge(norm_done, 2 * B)
            for t in range(TILES):
                pe.transpose(tile[t], attn[:, t].rearrange("p o h d -> p (o h d)"), ident[:]).then_inc(aT_ps_ok, 1)
            for t in range(TILES):
                pe.wait_ge(aT_ok, B + t)
                pe.matmul(tile[t], attnT[:, 128 * t:128 * t + 128], wT[:, 3], start=True, stop=True).then_inc(proj_ready, 1)
            for t in range(TILES):
                pe.wait_ge(ln_done, 2 * B - 1 + t)
                pe.transpose(tile[t], x1[:, t], ident[:]).then_inc(x1T_ps_ok, 1)
            pe.wait_ge(x1T_ok, B - 1 + TILES)
            for m in range(2):
                pe.matmul(s_ps[:, m], w1_sb[:, 128 * m:128 * m + 128], x1T, start=True, stop=True).then_inc(hid_ready, 1)
            for m in range(2):
                pe.wait_ge(relu_done, 2 * B - 1 + m)
                for t in range(TILES):
                    ins = pe.matmul(tile[t], hidT[:, m, 128 * t:128 * t + 128], w2_sb[:, m], start=(m == 0), stop=(m == 1))
                    if m:
                        ins.then_inc(y2_ready, 1)


_INS = ["L0_attn_x", "L0_attn_wq", "L0_attn_bq", "L0_attn_wk", "L0_attn_bk", "L0_attn_wv", "L0_attn_bv", "L0_attn_wo",
        "L0_attn_bo", "L0_attn_rot_cos", "L0_attn_rot_sin", "L0_ffn_W1", "L0_ffn_b1", "L0_ffn_W2", "L0_ffn_b2"]


def kernel(**inputs):
    import numpy as _np
    import concourse.bacc as _bacc
    from concourse import mybir as _mybir
    from concourse.bass_utils import run_bass_kernel_spmd as _run

    nc = _bacc.Bacc("TRN2", target_bir_lowering=False, num_devices=1)
    arrays, args = {}, []
    for name in _INS:
        a = _np.ascontiguousarray(inputs[name])
        arrays[f"in_{name}"] = a
        args.append(nc.dram_tensor(f"in_{name}", a.shape, _mybir.dt.from_np(a.dtype), kind="ExternalInput").ap())
    args.append(nc.dram_tensor("out_0", (B, T, D), _mybir.dt.float32, kind="ExternalOutput").ap())
    build_layer(nc, *args)
    r = _run(nc, [arrays], core_ids=[0])
    return r.results[0]["out_0"]
```
